# Optimizing a Trainium2 kernel written in Bass

```python
import numpy as np
import jax
import jax.numpy as jnp

def _softmax(x, axis=-1):
    return jax.nn.softmax(x, axis=axis)

def _gelu(x):
    return jax.nn.gelu(x, approximate=True)

def _silu(x):
    return jax.nn.silu(x)

def _sigmoid(x):
    return jax.nn.sigmoid(x)

def _layernorm(x, axis=-1, eps=1e-05):
    m = jnp.mean(x, axis=axis, keepdims=True)
    v = jnp.var(x, axis=axis, keepdims=True)
    return (x - m) / jnp.sqrt(v + eps)

def _scatter_add(tgt, idx, src, axis=0):
    return tgt.at[idx].add(src)

def _segment_sum(src, seg, n):
    return jax.ops.segment_sum(src, seg, n)
kernel_name = 'mk_adj_ffn_d4_adj_r2_8b2232'

def setup_inputs(seed: int=0):
    np.random.seed(seed)
    _w = jnp.asarray

    def _rec_inputs():
        import jax
        import jax.numpy as jnp
        _gk = jax.random.key(seed)
        x = 7.22e-05 + 1 * jax.random.normal(jax.random.fold_in(_gk, 1), (64, 128, 128), jnp.float32)
        _w = (1.0 + jnp.arange(128, dtype=jnp.float32)) ** (-0.5)
        _w = _w / _w.mean()
        _pij = jnp.clip(0.125 * _w[:, None] * _w[None, :], 0.0, 1.0)
        _a = jax.random.uniform(jax.random.fold_in(_gk, 2), (64, 128, 128)) < _pij
        _a = jnp.logical_or(_a, jnp.swapaxes(_a, -1, -2))
        _a = jnp.logical_or(_a, jnp.eye(128, dtype=bool))
        _af = _a.astype(jnp.float32)
        _af = _af * jax.random.uniform(jax.random.fold_in(_gk, 3), (64, 128, 128), jnp.float32, 0.05, 1)
        adj = _af
        return (x, adj)
    x, adj = _rec_inputs()

    def _L0_gnn_setup():
        import jax, jax.numpy as jnp
        import numpy as np
        B, K, H = (32, 512, 128)
        LN_EPS = 1e-05

        def layer_norm(x, gamma, beta):
            mu = jnp.mean(x, axis=-1, keepdims=True)
            var = jnp.mean(jnp.square(x - mu), axis=-1, keepdims=True)
            return (x - mu) * jax.lax.rsqrt(var + LN_EPS) * gamma + beta
        key = jax.random.key(seed)
        k1, k2, k3, k4 = jax.random.split(key, 4)
        x = jax.random.normal(k1, (B, K, H), dtype=jnp.float32)
        adj = jax.random.uniform(k2, (B, K, K), dtype=jnp.float32)
        s = 1.0 / np.sqrt(H)
        W_rel = jax.random.normal(k3, (H, H), dtype=jnp.float32) * s
        b_rel = jnp.zeros((H,), dtype=jnp.float32)
        W_root = jax.random.normal(k4, (H, H), dtype=jnp.float32) * s
        ln_gamma = jnp.ones((H,), dtype=jnp.float32)
        ln_beta = jnp.zeros((H,), dtype=jnp.float32)
        return {'x': x, 'adj': adj, 'W_rel': W_rel, 'b_rel': b_rel, 'W_root': W_root, 'ln_gamma': ln_gamma, 'ln_beta': ln_beta}
    _L0_gnn_all = _L0_gnn_setup()
    _L0_gnn_in = {k: v for k, v in _L0_gnn_all.items() if k in ('W_rel', 'b_rel', 'W_root', 'ln_gamma', 'ln_beta')}
    del _L0_gnn_all

    def _L0_ffn_setup():
        import jax, jax.numpy as jnp
        import numpy as np
        from jax import lax
        key = jax.random.key(seed)
        B, T, I, H = (64, 1024, 128, 128)
        ks = jax.random.split(key, 13)
        s = 1.0 / np.sqrt(H)

        def w(k, shape):
            return jax.random.uniform(k, shape, jnp.float32, -s, s)
        return {'x': jax.random.normal(ks[0], (B, T, I), jnp.float32), 'U_i': w(ks[1], (I, H)), 'V_i': w(ks[2], (H, H)), 'b_i': w(ks[3], (H,)), 'U_f': w(ks[4], (I, H)), 'V_f': w(ks[5], (H, H)), 'b_f': w(ks[6], (H,)), 'U_c': w(ks[7], (I, H)), 'V_c': w(ks[8], (H, H)), 'b_c': w(ks[9], (H,)), 'U_o': w(ks[10], (I, H)), 'V_o': w(ks[11], (H, H)), 'b_o': w(ks[12], (H,))}
    _L0_ffn_all = _L0_ffn_setup()
    _L0_ffn_in = {k: v for k, v in _L0_ffn_all.items() if k in ('U_i', 'V_i', 'b_i', 'U_f', 'V_f', 'b_f', 'U_c', 'V_c', 'b_c', 'U_o', 'V_o', 'b_o')}
    del _L0_ffn_all

    def _L1_gnn_setup():
        import jax, jax.numpy as jnp
        import numpy as np
        B, N, F_IN, F_OUT = (32, 512, 128, 128)
        EPS = 1e-08
        key = jax.random.key(seed)
        k1, k2, k3 = jax.random.split(key, 3)
        x = jax.random.normal(k1, (B, N, F_IN), dtype=jnp.float32)
        adj = jax.random.uniform(k2, (B, N, N), dtype=jnp.float32)
        fan_in, fan_out = (2 * F_IN, F_OUT)
        limit = float(np.sqrt(6.0 / (fan_in + fan_out)))
        weight = jax.random.uniform(k3, (2 * F_IN, F_OUT), minval=-limit, maxval=limit, dtype=jnp.float32)
        bias = jnp.zeros((F_OUT,), dtype=jnp.float32)
        return {'x': x, 'adj': adj, 'weight': weight, 'bias': bias}
    _L1_gnn_all = _L1_gnn_setup()
    _L1_gnn_in = {k: v for k, v in _L1_gnn_all.items() if k in ('weight', 'bias')}
    del _L1_gnn_all

    def _L1_ffn_setup():
        import math
        import jax, jax.numpy as jnp
        import numpy as np
        CAPACITY_FACTOR = 1.25
        TOP_K = 2
        LN_EPS = 1e-05

        def _layer_norm(x, gamma, beta):
            mu = jnp.mean(x, axis=-1, keepdims=True)
            var = jnp.var(x, axis=-1, keepdims=True)
            return (x - mu) * jax.lax.rsqrt(var + LN_EPS) * gamma + beta
        key = jax.random.key(seed)
        ks = jax.random.split(key, 4)
        B, S, D, F, E = (8, 2048, 128, 256, 8)
        x = jax.random.normal(ks[0], (B, S, D), dtype=jnp.float32)
        Wr = jax.random.normal(ks[1], (D, E), dtype=jnp.float32) / np.sqrt(D)
        br = jnp.zeros((E,), jnp.float32)
        W1 = jax.random.normal(ks[2], (E, D, F), dtype=jnp.float32) / np.sqrt(D)
        b1 = jnp.zeros((E, F), jnp.float32)
        W2 = jax.random.normal(ks[3], (E, F, D), dtype=jnp.float32) / np.sqrt(F)
        b2 = jnp.zeros((E, D), jnp.float32)
        gamma = jnp.ones((D,), jnp.float32)
        beta = jnp.zeros((D,), jnp.float32)
        return {'x': x, 'Wr': Wr, 'br': br, 'W1': W1, 'b1': b1, 'W2': W2, 'b2': b2, 'gamma': gamma, 'beta': beta}
    _L1_ffn_all = _L1_ffn_setup()
    _L1_ffn_in = {k: v for k, v in _L1_ffn_all.items() if k in ('Wr', 'br', 'W1', 'b1', 'W2', 'b2', 'gamma', 'beta')}
    del _L1_ffn_all

    def _L2_gnn_setup():
        import math
        import jax, jax.numpy as jnp
        import numpy as np
        HIDDEN = 128
        HEADS = 8
        HEAD_DIM = HIDDEN // HEADS
        key = jax.random.key(seed)
        ks = jax.random.split(key, 8)
        b, n = (2, 2048)
        node_state = jax.random.normal(ks[0], (b, n, HIDDEN), dtype=jnp.float32)
        adjacency = jax.random.uniform(ks[1], (b, n, n), dtype=jnp.float32)
        s = 1.0 / math.sqrt(HIDDEN)
        Wq = jax.random.uniform(ks[2], (HIDDEN, HIDDEN), jnp.float32, -s, s)
        Wk = jax.random.uniform(ks[3], (HIDDEN, HIDDEN), jnp.float32, -s, s)
        Wv = jax.random.uniform(ks[4], (HIDDEN, HIDDEN), jnp.float32, -s, s)
        Wo = jax.random.uniform(ks[5], (HIDDEN, HIDDEN), jnp.float32, -s, s)
        bo = jax.random.uniform(ks[6], (HIDDEN,), jnp.float32, -s, s)
        return {'node_state': node_state, 'adjacency': adjacency, 'Wq': Wq, 'Wk': Wk, 'Wv': Wv, 'Wo': Wo, 'bo': bo}
    _L2_gnn_all = _L2_gnn_setup()
    _L2_gnn_in = {k: v for k, v in _L2_gnn_all.items() if k in ('Wq', 'Wk', 'Wv', 'Wo', 'bo')}
    del _L2_gnn_all

    def _L2_ffn_setup():
        import jax, jax.numpy as jnp
        import numpy as np
        B, S, D, F, E, K = (8, 1024, 128, 512, 8, 2)
        key = jax.random.key(seed)
        ks = jax.random.split(key, 10)
        s = 0.02
        return {'x': jax.random.normal(ks[0], (B, S, D), dtype=jnp.float32), 'Wr': jax.random.normal(ks[1], (D, E), dtype=jnp.float32) * s, 'W1s': jax.random.normal(ks[2], (D, F), dtype=jnp.float32) * s, 'b1s': jnp.zeros((F,), dtype=jnp.float32), 'W2s': jax.random.normal(ks[3], (F, D), dtype=jnp.float32) * s, 'b2s': jnp.zeros((D,), dtype=jnp.float32), 'W1p': jax.random.normal(ks[4], (E, D, F), dtype=jnp.float32) * s, 'b1p': jnp.zeros((E, F), dtype=jnp.float32), 'W2p': jax.random.normal(ks[5], (E, F, D), dtype=jnp.float32) * s, 'b2p': jnp.zeros((E, D), dtype=jnp.float32)}
    _L2_ffn_all = _L2_ffn_setup()
    _L2_ffn_in = {k: v for k, v in _L2_ffn_all.items() if k in ('Wr', 'W1s', 'b1s', 'W2s', 'b2s', 'W1p', 'b1p', 'W2p', 'b2p')}
    del _L2_ffn_all

    def _L3_gnn_setup():
        import jax, jax.numpy as jnp
        import numpy as np
        SPARSITY = 0.01

        def quantize(weight, s):
            pos = (weight > s).astype(weight.dtype)
            neg = (weight < -s).astype(weight.dtype)
            return (pos - neg) * s
        key = jax.random.key(seed)
        k1, k2, k3 = jax.random.split(key, 3)
        B, N, Din, Dout = (8, 1024, 128, 128)
        x = jax.random.normal(k1, (B, N, Din), dtype=jnp.float32)
        adj = jax.random.uniform(k2, (B, N, N), dtype=jnp.float32)
        limit = float(np.sqrt(6.0 / (Din + Dout)))
        weight = jax.random.uniform(k3, (Din, Dout), dtype=jnp.float32, minval=-limit, maxval=limit)
        bias = jnp.zeros((Dout,), dtype=jnp.float32)
        return {'x': x, 'adj': adj, 'weight': weight, 'bias': bias}
    _L3_gnn_all = _L3_gnn_setup()
    _L3_gnn_in = {k: v for k, v in _L3_gnn_all.items() if k in ('weight', 'bias')}
    del _L3_gnn_all

    def _L3_ffn_setup():
        import jax, jax.numpy as jnp
        import numpy as np
        B, K, D = (256, 16, 128)
        E = 32
        H = int(D * 0.25)
        key = jax.random.key(seed)
        ks = jax.random.split(key, 7)
        d_rs = D ** (-0.5)
        h_rs = H ** (-0.5)
        x = jax.random.normal(ks[0], (B, K, D), dtype=jnp.float32)
        router_w = jax.random.uniform(ks[1], (E, D), jnp.float32, -d_rs, d_rs)
        router_b = jax.random.uniform(ks[2], (E,), jnp.float32, -d_rs, d_rs)
        W1 = jax.random.uniform(ks[3], (E, D, H), jnp.float32, -h_rs, h_rs)
        b1 = jax.random.uniform(ks[4], (E, H), jnp.float32, -h_rs, h_rs)
        W2 = jax.random.uniform(ks[5], (E, H, D), jnp.float32, -d_rs, d_rs)
        b2 = jax.random.uniform(ks[6], (E, D), jnp.float32, -d_rs, d_rs)
        return {'x': x, 'router_w': router_w, 'router_b': router_b, 'W1': W1, 'b1': b1, 'W2': W2, 'b2': b2}
    _L3_ffn_all = _L3_ffn_setup()
    _L3_ffn_in = {k: v for k, v in _L3_ffn_all.items() if k in ('router_w', 'router_b', 'W1', 'b1', 'W2', 'b2')}
    del _L3_ffn_all
    return {'x': x, 'adj': adj, 'L0_gnn_W_rel': _L0_gnn_in['W_rel'], 'L0_gnn_b_rel': _L0_gnn_in['b_rel'], 'L0_gnn_W_root': _L0_gnn_in['W_root'], 'L0_gnn_ln_gamma': _L0_gnn_in['ln_gamma'], 'L0_gnn_ln_beta': _L0_gnn_in['ln_beta'], 'L0_ffn_U_i': _L0_ffn_in['U_i'], 'L0_ffn_V_i': _L0_ffn_in['V_i'], 'L0_ffn_b_i': _L0_ffn_in['b_i'], 'L0_ffn_U_f': _L0_ffn_in['U_f'], 'L0_ffn_V_f': _L0_ffn_in['V_f'], 'L0_ffn_b_f': _L0_ffn_in['b_f'], 'L0_ffn_U_c': _L0_ffn_in['U_c'], 'L0_ffn_V_c': _L0_ffn_in['V_c'], 'L0_ffn_b_c': _L0_ffn_in['b_c'], 'L0_ffn_U_o': _L0_ffn_in['U_o'], 'L0_ffn_V_o': _L0_ffn_in['V_o'], 'L0_ffn_b_o': _L0_ffn_in['b_o'], 'L1_gnn_weight': _L1_gnn_in['weight'], 'L1_gnn_bias': _L1_gnn_in['bias'], 'L1_ffn_Wr': _L1_ffn_in['Wr'], 'L1_ffn_br': _L1_ffn_in['br'], 'L1_ffn_W1': _L1_ffn_in['W1'], 'L1_ffn_b1': _L1_ffn_in['b1'], 'L1_ffn_W2': _L1_ffn_in['W2'], 'L1_ffn_b2': _L1_ffn_in['b2'], 'L1_ffn_gamma': _L1_ffn_in['gamma'], 'L1_ffn_beta': _L1_ffn_in['beta'], 'L2_gnn_Wq': _L2_gnn_in['Wq'], 'L2_gnn_Wk': _L2_gnn_in['Wk'], 'L2_gnn_Wv': _L2_gnn_in['Wv'], 'L2_gnn_Wo': _L2_gnn_in['Wo'], 'L2_gnn_bo': _L2_gnn_in['bo'], 'L2_ffn_Wr': _L2_ffn_in['Wr'], 'L2_ffn_W1s': _L2_ffn_in['W1s'], 'L2_ffn_b1s': _L2_ffn_in['b1s'], 'L2_ffn_W2s': _L2_ffn_in['W2s'], 'L2_ffn_b2s': _L2_ffn_in['b2s'], 'L2_ffn_W1p': _L2_ffn_in['W1p'], 'L2_ffn_b1p': _L2_ffn_in['b1p'], 'L2_ffn_W2p': _L2_ffn_in['W2p'], 'L2_ffn_b2p': _L2_ffn_in['b2p'], 'L3_gnn_weight': _L3_gnn_in['weight'], 'L3_gnn_bias': _L3_gnn_in['bias'], 'L3_ffn_router_w': _L3_ffn_in['router_w'], 'L3_ffn_router_b': _L3_ffn_in['router_b'], 'L3_ffn_W1': _L3_ffn_in['W1'], 'L3_ffn_b1': _L3_ffn_in['b1'], 'L3_ffn_W2': _L3_ffn_in['W2'], 'L3_ffn_b2': _L3_ffn_in['b2']}

def reference(x, adj, L0_gnn_W_rel, L0_gnn_b_rel, L0_gnn_W_root, L0_gnn_ln_gamma, L0_gnn_ln_beta, L0_ffn_U_i, L0_ffn_V_i, L0_ffn_b_i, L0_ffn_U_f, L0_ffn_V_f, L0_ffn_b_f, L0_ffn_U_c, L0_ffn_V_c, L0_ffn_b_c, L0_ffn_U_o, L0_ffn_V_o, L0_ffn_b_o, L1_gnn_weight, L1_gnn_bias, L1_ffn_Wr, L1_ffn_br, L1_ffn_W1, L1_ffn_b1, L1_ffn_W2, L1_ffn_b2, L1_ffn_gamma, L1_ffn_beta, L2_gnn_Wq, L2_gnn_Wk, L2_gnn_Wv, L2_gnn_Wo, L2_gnn_bo, L2_ffn_Wr, L2_ffn_W1s, L2_ffn_b1s, L2_ffn_W2s, L2_ffn_b2s, L2_ffn_W1p, L2_ffn_b1p, L2_ffn_W2p, L2_ffn_b2p, L3_gnn_weight, L3_gnn_bias, L3_ffn_router_w, L3_ffn_router_b, L3_ffn_W1, L3_ffn_b1, L3_ffn_W2, L3_ffn_b2):
    import jax
    import jax.numpy as jnp

    def _L0_gnn_ref(x, adj, W_rel, b_rel, W_root, ln_gamma, ln_beta):
        import jax, jax.numpy as jnp
        import numpy as np
        B, K, H = (32, 512, 128)
        LN_EPS = 1e-05

        def layer_norm(x, gamma, beta):
            mu = jnp.mean(x, axis=-1, keepdims=True)
            var = jnp.mean(jnp.square(x - mu), axis=-1, keepdims=True)
            return (x - mu) * jax.lax.rsqrt(var + LN_EPS) * gamma + beta
        h = layer_norm(x, ln_gamma, ln_beta)
        agg = jnp.einsum('bij,bjh->bih', adj, h)
        conv = jnp.einsum('bkh,ho->bko', agg, W_rel) + b_rel + jnp.einsum('bkh,ho->bko', h, W_root)
        return x + jax.nn.relu(conv)

    def _L0_ffn_ref(x, U_i, V_i, b_i, U_f, V_f, b_f, U_c, V_c, b_c, U_o, V_o, b_o):
        import jax, jax.numpy as jnp
        import numpy as np
        from jax import lax
        B, T, _ = x.shape
        H = U_i.shape[1]
        xt = jnp.swapaxes(x, 0, 1)
        xi = xt @ U_i + b_i
        xf = xt @ U_f + b_f
        xg = xt @ U_c + b_c
        xo = xt @ U_o + b_o
        h0 = jnp.zeros((B, H), x.dtype)
        c0 = jnp.zeros((B, H), x.dtype)

        def step(carry, xs):
            h, c = carry
            xi_t, xf_t, xg_t, xo_t = xs
            i_t = jax.nn.sigmoid(xi_t + h @ V_i)
            f_t = jax.nn.sigmoid(xf_t + h @ V_f)
            g_t = jnp.tanh(xg_t + h @ V_c)
            o_t = jax.nn.sigmoid(xo_t + h @ V_o)
            c_new = h * c + i_t * g_t
            h_new = o_t * jnp.tanh(c_new)
            return ((h_new, c_new), h_new)
        (_, _), hs = lax.scan(step, (h0, c0), (xi, xf, xg, xo))
        return jnp.swapaxes(hs, 0, 1)

    def _L1_gnn_ref(x, adj, weight, bias):
        import jax, jax.numpy as jnp
        import numpy as np
        B, N, F_IN, F_OUT = (32, 512, 128, 128)
        EPS = 1e-08
        adj_norm = adj / (jnp.sum(adj, axis=-1, keepdims=True) + EPS)
        h_neigh = jnp.einsum('bnm,bmf->bnf', adj_norm, x)
        h_concat = jnp.concatenate([x, h_neigh], axis=-1)
        h = jnp.einsum('bnk,ko->bno', h_concat, weight) + bias
        return jax.nn.relu(h)

    def _L1_ffn_ref(x, Wr, br, W1, b1, W2, b2, gamma, beta):
        import math
        import jax, jax.numpy as jnp
        import numpy as np
        CAPACITY_FACTOR = 1.25
        TOP_K = 2
        LN_EPS = 1e-05

        def _layer_norm(x, gamma, beta):
            mu = jnp.mean(x, axis=-1, keepdims=True)
            var = jnp.var(x, axis=-1, keepdims=True)
            return (x - mu) * jax.lax.rsqrt(var + LN_EPS) * gamma + beta
        B, S, D = x.shape
        E = Wr.shape[1]
        N = B * S
        K = TOP_K
        logits = jnp.mean(x, axis=1) @ Wr + br
        routing_weights = jax.nn.softmax(logits, axis=-1)
        capacity = float(math.ceil(N * CAPACITY_FACTOR / E))
        expected_loads = routing_weights.sum(axis=0) * (N / B)
        scale = jnp.where(expected_loads > capacity, capacity / expected_loads, 1.0)
        routing_weights = jax.nn.softmax(routing_weights * scale, axis=-1)
        rw_tok = jnp.broadcast_to(routing_weights[:, None, :], (B, S, E)).reshape(N, E)
        top_w, top_i = jax.lax.top_k(rw_tok, K)
        top_w = jax.nn.softmax(top_w, axis=-1)
        xf = x.reshape(N, D)
        h = jax.nn.gelu(jnp.einsum('nd,edf->enf', xf, W1) + b1[:, None, :], approximate=False)
        y = jnp.einsum('enf,efd->end', h, W2) + b2[:, None, :]
        w_dense = jnp.zeros((N, E), x.dtype).at[jnp.arange(N)[:, None], top_i].add(top_w)
        out = jnp.einsum('ne,end->nd', w_dense, y).reshape(B, S, D)
        out = _layer_norm(out + x, gamma, beta)
        return out

    def _L2_gnn_ref(node_state, adjacency, Wq, Wk, Wv, Wo, bo):
        import math
        import jax, jax.numpy as jnp
        import numpy as np
        HIDDEN = 128
        HEADS = 8
        HEAD_DIM = HIDDEN // HEADS
        b, n, _ = node_state.shape

        def split_heads(x):
            return x.reshape(b, n, HEADS, HEAD_DIM).transpose(0, 2, 1, 3)
        q = split_heads(node_state @ Wq.T)
        k = split_heads(node_state @ Wk.T)
        v = split_heads(node_state @ Wv.T)
        scores = jnp.einsum('bhqd,bhkd->bhqk', q, k) / math.sqrt(HEAD_DIM)
        log_adj = jnp.log(adjacency + 1e-06)
        scores = scores + log_adj[:, None, :, :]
        attn = jax.nn.softmax(scores, axis=-1)
        out = jnp.einsum('bhqk,bhkd->bhqd', attn, v)
        out = out.transpose(0, 2, 1, 3).reshape(b, n, HIDDEN)
        return out @ Wo.T + bo

    def _L2_ffn_ref(x, Wr, W1s, b1s, W2s, b2s, W1p, b1p, W2p, b2p):
        import jax, jax.numpy as jnp
        import numpy as np
        B, S, D, F, E, K = (8, 1024, 128, 512, 8, 2)
        gelu = lambda t: jax.nn.gelu(t, approximate=False)
        shared = gelu(x @ W1s + b1s) @ W2s + b2s
        rw = jax.nn.softmax(x @ Wr, axis=-1)
        topw, topi = jax.lax.top_k(rw, K)
        topw = topw / jnp.sum(topw, axis=-1, keepdims=True)
        mask = jnp.sum(jax.nn.one_hot(topi, E, dtype=topw.dtype) * topw[..., None], axis=-2)
        h = gelu(jnp.einsum('bsd,edf->bsef', x, W1p) + b1p)
        priv = jnp.einsum('bsef,efd->bsed', h, W2p) + b2p
        routed = jnp.einsum('bsed,bse->bsd', priv, mask)
        return shared + routed

    def _L3_gnn_ref(x, adj, weight, bias):
        import jax, jax.numpy as jnp
        import numpy as np
        SPARSITY = 0.01

        def quantize(weight, s):
            pos = (weight > s).astype(weight.dtype)
            neg = (weight < -s).astype(weight.dtype)
            return (pos - neg) * s
        dw = quantize(weight, SPARSITY)
        support = jnp.einsum('bni,io->bno', x, dw)
        out = jnp.einsum('bnm,bmo->bno', adj, support) + bias
        return jax.nn.relu(out)

    def _L3_ffn_ref(x, router_w, router_b, W1, b1, W2, b2):
        import jax, jax.numpy as jnp
        import numpy as np
        B, K, D = (256, 16, 128)
        E = 32
        H = int(D * 0.25)
        xf = x.reshape(-1, D)
        logits = xf @ router_w.T + router_b
        idx = jnp.argmax(logits, axis=-1)
        w1t = jnp.take(W1, idx, axis=0)
        h = jnp.einsum('nd,ndh->nh', xf, w1t) + jnp.take(b1, idx, axis=0)
        h = jax.nn.relu(h)
        w2t = jnp.take(W2, idx, axis=0)
        out = jnp.einsum('nh,nhd->nd', h, w2t) + jnp.take(b2, idx, axis=0)
        out = jax.nn.relu(out)
        return out.reshape(x.shape)
    x = x + _L0_gnn_ref(_layernorm(x, axis=-1), adj, L0_gnn_W_rel, L0_gnn_b_rel, L0_gnn_W_root, L0_gnn_ln_gamma, L0_gnn_ln_beta)
    x = x + _L0_ffn_ref(_layernorm(x, axis=-1), L0_ffn_U_i, L0_ffn_V_i, L0_ffn_b_i, L0_ffn_U_f, L0_ffn_V_f, L0_ffn_b_f, L0_ffn_U_c, L0_ffn_V_c, L0_ffn_b_c, L0_ffn_U_o, L0_ffn_V_o, L0_ffn_b_o)
    x = x + _L1_gnn_ref(_layernorm(x, axis=-1), adj, L1_gnn_weight, L1_gnn_bias)
    x = x + _L1_ffn_ref(_layernorm(x, axis=-1), L1_ffn_Wr, L1_ffn_br, L1_ffn_W1, L1_ffn_b1, L1_ffn_W2, L1_ffn_b2, L1_ffn_gamma, L1_ffn_beta)
    x = x + _L2_gnn_ref(_layernorm(x, axis=-1), adj, L2_gnn_Wq, L2_gnn_Wk, L2_gnn_Wv, L2_gnn_Wo, L2_gnn_bo)
    x = x + _L2_ffn_ref(_layernorm(x, axis=-1), L2_ffn_Wr, L2_ffn_W1s, L2_ffn_b1s, L2_ffn_W2s, L2_ffn_b2s, L2_ffn_W1p, L2_ffn_b1p, L2_ffn_W2p, L2_ffn_b2p)
    x = x + _L3_gnn_ref(_layernorm(x, axis=-1), adj, L3_gnn_weight, L3_gnn_bias)
    x = x + _L3_ffn_ref(_layernorm(x, axis=-1), L3_ffn_router_w, L3_ffn_router_b, L3_ffn_W1, L3_ffn_b1, L3_ffn_W2, L3_ffn_b2)
    return x

_drawn_inputs = setup_inputs


def setup_inputs(seed=0):
    import zlib

    import numpy as np

    out = dict(_drawn_inputs(seed))
    spreads = {'L0_gnn_b_rel': (0.0, 0.1),
     'L0_gnn_ln_gamma': (1.0, 0.2),
     'L0_gnn_ln_beta': (0.0, 0.1),
     'L1_gnn_bias': (0.0, 0.27),
     'L1_ffn_br': (0.0, 0.1),
     'L1_ffn_b1': (0.0, 0.706),
     'L1_ffn_b2': (0.0, 0.5),
     'L1_ffn_gamma': (1.0, 0.2),
     'L1_ffn_beta': (0.0, 0.344),
     'L2_ffn_b1s': (0.0, 0.8),
     'L2_ffn_b2s': (0.0, 0.365),
     'L2_ffn_b1p': (0.0, 0.8),
     'L2_ffn_b2p': (0.0, 0.455),
     'L3_gnn_bias': (0.0, 0.51)}
    factors = {'L0_ffn_U_i': 3.643,
     'L0_ffn_V_i': 8.0,
     'L0_ffn_b_i': 8.0,
     'L0_ffn_V_c': 8.0,
     'L0_ffn_b_c': 4.358,
     'L0_ffn_U_o': 3.562,
     'L0_ffn_V_o': 8.0,
     'L0_ffn_b_o': 8.0,
     'L2_gnn_Wq': 8.0,
     'L2_gnn_Wk': 8.0,
     'L2_gnn_bo': 4.267,
     'L2_ffn_Wr': 3.35,
     'L2_ffn_W1s': 4.494,
     'L2_ffn_W2s': 4.066,
     'L2_ffn_W1p': 6.198,
     'L2_ffn_W2p': 5.64,
     'L3_ffn_router_b': 4.657,
     'L3_ffn_b1': 23.829,
     'L3_ffn_b2': 7.606}
    for name, (base, spread) in spreads.items():
        noise = np.random.default_rng([zlib.crc32(name.encode()), seed]).standard_normal(out[name].shape)
        drawn = base * np.exp(spread * noise) if base else spread * noise
        out[name] = jnp.asarray(drawn.astype(out[name].dtype))
    for name, factor in factors.items():
        out[name] = (out[name] * factor).astype(out[name].dtype)
    return out
```

```python
import concourse.bass as bass
from concourse import mybir
from contextlib import ExitStack

FP32 = mybir.dt.float32
INT32 = mybir.dt.int32
UINT32 = mybir.dt.uint32
ALU = mybir.AluOpType
ACT = mybir.ActivationFunctionType
AX = mybir.AxisListType

P = 128
B, T, H = 64, 128, 128
G = 4
NG = B // G
GW = G * T
EPS = 1e-5
DENOM_EPS = 1e-8
ADJ_EPS = 1e-6
E1, F1 = 8, 256
C1 = F1 // P
HEADS = 8
HD = H // HEADS
HP = 32
HC = P // HP
NC = HEADS // HC
E2, F2 = 8, 512
C2 = F2 // P
E3, F3 = 32, 32
C3 = E3 * F3 // P
EC3 = E3 // C3
SPARSITY = 0.01
CAPACITY = float(-(-B * T * 5 // (4 * E1)))
STEPS = 8


def pipelined(eng, n, parts):
    depth = max(lag for lag, _ in parts)
    first = depth + 2 + depth % 2

    def one(j):
        for lag, emit in parts:
            if 0 <= j - lag < n:
                emit(j - lag, (j - lag) % 2, (j - lag) // 2)

    for j in range(first):
        one(j)
    with eng.Fori(first // 2, n // 2) as half:
        for u in range(2):
            for lag, emit in parts:
                emit(2 * half + (u - lag), (u - lag) % 2, half + (u - lag) // 2)
    for j in range(n, n + depth):
        one(j)


def reused(eng, sem, i, lag, per=1):
    if isinstance(i, int) and i < lag:
        return
    eng.wait_ge(sem, (i - (lag - 1)) * per)


def program(nc, a, out):
    ctx = ExitStack()
    with ctx:
        def sb(name, shape, dt=FP32):
            return ctx.enter_context(nc.sbuf_tensor(name, shape, dt))

        layers = [ExitStack()]

        def layer():
            layers.pop().close()
            layers.append(ExitStack())

        def lb(name, shape, dt=FP32):
            return layers[0].enter_context(nc.sbuf_tensor(name, shape, dt))

        held = []

        def release():
            if held:
                nc.clear_and_free_semaphores(held)
                nc.all_engine_barrier()
                held.clear()

        def sems(phase, names):
            release()
            held.extend(nc.alloc_semaphore(name=f"{phase}_{n}") for n in names.split())
            return type("Signals", (), dict(zip(names.split(), held)))

        X = sb("X", [P, B * H])
        AT = sb("AT", [P, B * T])
        FEAT = sb("FEAT", [P, B * T])
        AUX = sb("AUX", [P, B * T + B])
        EXP = sb("EXP", [P, 6144])
        BANKS = ctx.enter_context(nc.psum_tensor("BANKS", [P, 8, 512], FP32))
        PS = [BANKS[:, k, :] for k in range(8)]

        ident = sb("ident", [P, P])
        ones = sb("ones", [P, P])
        iota8 = sb("iota8", [P, 8])
        mhalf = sb("mhalf", [P, G])
        epsilon = sb("epsilon", [P, G])
        STAGE = sb("STAGE", [P, 2, GW])
        STATS = sb("STATS", [P, 2, G, 6])
        MV = sb("MV", [P, 2, G, 2])
        RS = sb("RS", [P, 2, 5, G])
        STATSB = sb("STATSB", [P, 2, G, 6])
        MVB = sb("MVB", [P, 2, G, 2])
        RSB = sb("RSB", [P, 2, 2, G])
        WA = sb("WA", [P, 2, GW])
        WB = sb("WB", [P, 2, GW])
        WC = sb("WC", [P, 2, GW])
        WD = sb("WD", [P, 2, GW])
        WC2 = sb("WC2", [P, 2, GW])
        WF = sb("WF", [P, 2, GW])
        WE = sb("WE", [P, 2, GW])

        def cols(t, i, w=GW, at=0, n=None):
            n = w if n is None else n
            return t[:, i * w + at:i * w + at + n] if isinstance(i, int) else t[:, bass.ds(i * w + at, n)]

        def tile(t, k):
            return t[:, k * T:(k + 1) * T]

        weights = {}
        w_shapes = dict(rel=(H, H), root=(H, H), g0=(H, 1), be0=(H, 1), b0=(H, 1))

        def weight(name, shape, src, eng, sem):
            weights[name] = lb("w_" + name, shape)
            eng.dma_start(weights[name][:], src).then_inc(sem, 16)

        def column(v):
            return v.rearrange("(p a) -> p a", a=1)

        setup = type("Signals", (), {n: ctx.enter_context(nc.semaphore("setup_" + n)) for n in ("zero", "const", "load")})

        def wait_apart(eng, sem, value):
            value = value if isinstance(value, int) else eng.to_reg(value)
            eng.wait_ge(setup.const, 1)
            eng.wait_ge(sem, value)

        def statistics(v, i, par, stats, mv, s_raw, s_mv):
            for k in range(G):
                last = v.bn_stats(stats[:, par, k, :], cols(X, i, GW, k * H, H))
            last.then_inc(s_raw, 1)
            wait_apart(v, s_raw, i + 1)
            for k in range(G):
                last = v.bn_aggr(mv[:, par, k, :], stats[:, par, k, :])
            last.then_inc(s_mv, 1)

        def inverse_deviation(pool, i, par, mv, rs, s_mv, s_var, s_rstd):
            pool.wait_ge(s_mv, i + 1)
            pool.tensor_tensor(rs[:, par, 0, :], mv[:, par, :, 1], epsilon[:], ALU.add).then_inc(s_var, 1)
            pool.wait_ge(s_var, i + 1)
            pool.tensor_tensor(rs[:, par, 1, :], rs[:, par, 0, :], mhalf[:], ALU.pow).then_inc(s_rstd, 1)

        def normalise(v, i, par, dst, mv, rs, row, s_done):
            for k in range(G):
                last = v.tensor_scalar(tile(dst[:, par], k), cols(X, i, GW, k * H, H), mv[:, par, k, 0:1],
                                       rs[:, par, row, k:k + 1], ALU.subtract, ALU.mult)
            last.then_inc(s_done, 1)

        def transpose4(pe, ps, src, s_done):
            for k in range(G):
                last = pe.transpose(tile(ps, k), tile(src, k), ident[:])
            last.then_inc(s_done, 1)

        s = setup
        load0 = s.load
        with nc.Block() as block:
            @block.gpsimd
            def _(pool):
                pool.memset(ident[:], 0.0).then_inc(s.zero, 1)
                pool.memset(ones[:], 1.0)
                pool.iota(iota8[:], [[1, 8]], base=0, channel_multiplier=0, allow_small_or_imprecise_dtypes=True)
                pool.memset(mhalf[:], -0.5)
                pool.memset(epsilon[:], EPS)
                pool.wait_ge(s.zero, 1)
                pool.affine_select(out=ident[:], in_=ident[:], compare_op=ALU.not_equal, fill=1.0, base=0,
                                   pattern=[[-1, P]], channel_multiplier=1).then_inc(s.const, 1)

            @block.sync
            def _(sp):
                weight("rel", [H, H], a["L0_gnn_W_rel"], sp, load0)
                weight("root", [H, H], a["L0_gnn_W_root"], sp, load0)
                weight("g0", [H, 1], column(a["L0_gnn_ln_gamma"]), sp, load0)
                weight("be0", [H, 1], column(a["L0_gnn_ln_beta"]), sp, load0)
                weight("b0", [H, 1], column(a["L0_gnn_b_rel"]), sp, load0)
        N0 = 5 * 16
        W = weights

        s = sems("l0", "in0 in1 adjT_ps adjT raw mv var rstd t1 t2 t3 t3b t4 r2 xn x1 h_ps hT hw_ps hw conv relu back x2 "
                       "raw2 mv2 var2 rstd2 xn2 x_ps xT")
        adj_v = a["adj"].rearrange("(g b) i j -> g i b j", b=G)
        x_v = a["x"].rearrange("(g b) t h -> g t b h", b=G)

        def dgroup(v, i):
            return v[i] if isinstance(i, int) else v[bass.ds(i, 1)].rearrange("a p b c -> (a p) b c")

        with nc.Block() as block:
            @block.sync
            def _(sp):
                def load(i, par, half):
                    reused(sp, s.adjT_ps, i, 2)
                    sin = (s.in0, s.in1)[par]
                    sp.dma_start(STAGE[:, par].rearrange("p (b j) -> p b j", b=G), dgroup(adj_v, i)).then_inc(sin, 16)
                    sp.dma_start(cols(X, i).rearrange("p (b j) -> p b j", b=G), dgroup(x_v, i)).then_inc(sin, 16)
                pipelined(sp, NG, [(0, load)])

            @block.vector
            def _(v):
                def stats(i, par, half):
                    wait_apart(v, (s.in0, s.in1)[par], 32 * half + 32)
                    statistics(v, i, par, STATS, MV, s.raw, s.mv)

                def norm(i, par, half):
                    v.wait_ge(s.r2, i + 1)
                    reused(v, s.h_ps, i, 2)
                    normalise(v, i, par, WA, MV, RS, 4, s.xn)
                    normalise(v, i, par, WC, MV, RS, 1, s.t4)
                    v.wait_ge(s.t4, i + 1)
                    v.tensor_tensor(cols(X, i), cols(X, i), WC[:, par], ALU.add).then_inc(s.x1, 1)

                def add(i, par, half):
                    v.wait_ge(s.back, i + 1)
                    v.wait_ge(s.x1, i + 1)
                    v.tensor_tensor(cols(X, i), cols(X, i), PS[4], ALU.add).then_inc(s.x2, 1)
                    wait_apart(v, s.x2, i + 1)
                    statistics(v, i, par, STATSB, MVB, s.raw2, s.mv2)

                def norm2(i, par, half):
                    v.wait_ge(s.rstd2, i + 1)
                    reused(v, s.x_ps, i, 2)
                    normalise(v, i, par, WE, MVB, RSB, 1, s.xn2)
                pipelined(v, NG, [(3, norm2), (1, norm), (0, stats), (2, add)])

            @block.gpsimd
            def _(pool):
                def dev(i, par, half):
                    inverse_deviation(pool, i, par, MV, RS, s.mv, s.var, s.rstd)
                    pool.wait_ge(s.rstd, i + 1)
                    pool.tensor_tensor(RS[:, par, 2, :], MV[:, par, :, 1], RS[:, par, 1, :], ALU.mult).then_inc(s.t1, 1)
                    pool.wait_ge(s.t1, i + 1)
                    pool.tensor_tensor(RS[:, par, 3, :], RS[:, par, 2, :], RS[:, par, 1, :], ALU.mult).then_inc(s.t2, 1)
                    pool.wait_ge(s.t2, i + 1)
                    pool.tensor_tensor(RS[:, par, 2, :], RS[:, par, 3, :], epsilon[:], ALU.add).then_inc(s.t3, 1)
                    pool.wait_ge(s.t3, i + 1)
                    pool.tensor_tensor(RS[:, par, 3, :], RS[:, par, 2, :], mhalf[:], ALU.pow).then_inc(s.t3b, 1)
                    pool.wait_ge(s.t3b, i + 1)
                    pool.tensor_tensor(RS[:, par, 4, :], RS[:, par, 3, :], RS[:, par, 1, :], ALU.mult).then_inc(s.r2, 1)

                def dev2(i, par, half):
                    inverse_deviation(pool, i, par, MVB, RSB, s.mv2, s.var2, s.rstd2)
                pipelined(pool, NG, [(0, dev), (2, dev2)])

            @block.tensor
            def _(pe):
                def adjacency(i, par, half):
                    pe.wait_ge((s.in0, s.in1)[par], 32 * half + 32)
                    reused(pe, s.adjT, i, 1)
                    transpose4(pe, PS[0], STAGE[:, par], s.adjT_ps)

                def hT(i, par, half):
                    pe.wait_ge(s.xn, i + 1)
                    reused(pe, s.hT, i, 1)
                    transpose4(pe, PS[1], WA[:, par], s.h_ps)

                def project(i, par, half):
                    pe.wait_ge(s.hT, i + 1)
                    reused(pe, s.hw, i, 1)
                    for k in range(G):
                        last = pe.matmul(tile(PS[2], k), tile(WB[:, par], k), W["rel"][:], start=True, stop=True)
                    last.then_inc(s.hw_ps, 1)

                def conv(i, par, half):
                    reused(pe, s.relu, i, 1)
                    pe.matmul(PS[3], W["root"][:], WB[:, par], start=True, stop=False, skip_group_check=True)
                    pe.wait_ge(s.hw, i + 1)
                    pe.wait_ge(s.adjT, i + 1)
                    for k in range(G):
                        last = pe.matmul(tile(PS[3], k), tile(WC2[:, par], k), cols(AT, i, GW, k * T, T),
                                         start=False, stop=True, skip_group_check=True)
                    last.then_inc(s.conv, 1)

                def back(i, par, half):
                    pe.wait_ge(s.relu, i + 1)
                    reused(pe, s.x2, i, 1)
                    transpose4(pe, PS[4], WD[:, par], s.back)

                def xT(i, par, half):
                    pe.wait_ge(s.xn2, i + 1)
                    reused(pe, s.xT, i, 1)
                    transpose4(pe, PS[5], WE[:, par], s.x_ps)
                pe.wait_ge(load0, N0)
                pipelined(pe, NG, [(2, conv), (1, hT), (0, adjacency), (2, back), (1, project), (3, xT)])

            FEAT_v = FEAT[:].rearrange("p (t b) -> p b t", b=B)

            @block.scalar
            def _(act):
                def adjT(i, par, half):
                    act.wait_ge(s.adjT_ps, i + 1)
                    act.copy(cols(AT, i), PS[0]).then_inc(s.adjT, 1)

                def hT(i, par, half):
                    act.wait_ge(s.h_ps, i + 1)
                    reused(act, s.conv, i, 2)
                    act.activation(WB[:, par], PS[1], ACT.Identity, scale=W["g0"][:], bias=W["be0"][:]).then_inc(s.hT, 1)

                def hw(i, par, half):
                    act.wait_ge(s.hw_ps, i + 1)
                    act.copy(WC2[:, par], PS[2]).then_inc(s.hw, 1)

                def relu(i, par, half):
                    act.wait_ge(s.conv, i + 1)
                    reused(act, s.back, i, 2)
                    act.activation(WD[:, par], PS[3], ACT.Relu, bias=W["b0"][:]).then_inc(s.relu, 1)

                def xT(i, par, half):
                    act.wait_ge(s.x_ps, i + 1)
                    dst = FEAT_v[:, G * i:G * i + G, :] if isinstance(i, int) else FEAT_v[:, bass.ds(i * G, G), :]
                    act.copy(dst, PS[5].rearrange("p (b t) -> p b t", b=G)).then_inc(s.xT, 1)
                act.wait_ge(load0, N0)
                pipelined(act, NG, [(2, relu), (1, hT), (0, adjT), (1, hw), (3, xT)])

        layer()
        s = sems("rnn", "zero x_even x_odd g i o gt it ot hc ig c ct h w")
        wr = {}
        for gate in "cio":
            for mat in "UV":
                wr[mat + gate] = lb(f"w_{mat}{gate}", [H, H])
            wr["b" + gate] = lb(f"w_b{gate}", [H, 1])
        HS = AUX
        cell = lb("cell", [P, 2, B])
        hc = lb("hc", [P, 2, B])
        ig = lb("ig", [P, 2, B])
        gates = lb("gates", [P, 3, 2, B])
        tanhc = lb("tanhc", [P, 2, B])
        NT = T // STEPS
        with nc.Block() as block:
            @block.sync
            def _(sp):
                for gate in "cio":
                    sp.dma_start(wr["U" + gate][:], a["L0_ffn_U_" + gate]).then_inc(s.w, 16)
                    sp.dma_start(wr["V" + gate][:], a["L0_ffn_V_" + gate]).then_inc(s.w, 16)
                    sp.dma_start(wr["b" + gate][:], column(a["L0_ffn_b_" + gate])).then_inc(s.w, 16)

            @block.gpsimd
            def _(pool):
                pool.memset(HS[:, 0:B], 0.0).then_inc(s.zero, 1)
                pool.memset(cell[:, 1, :], 0.0).then_inc(s.zero, 1)

            @block.tensor
            def _(pe):
                half = STEPS * B // 2

                def inputs(j, par, gate_at, part):
                    gate = "ico"[gate_at]
                    pe.matmul(PS[2 * gate_at + par][:, part * half:(part + 1) * half], wr["U" + gate][:],
                              cols(FEAT, j, STEPS * B, part * half, half), start=(part == 0), stop=False,
                              skip_group_check=True)

                def turn(j, par, prefetch):
                    for u in range(STEPS):
                        step = j * STEPS + u
                        pe.wait_ge(s.h if not (isinstance(j, int) and step == 0) else s.zero,
                                   step if not (isinstance(j, int) and step == 0) else 2)
                        for gate_at, (gate, sem) in enumerate(zip("ico", (s.i, s.g, s.o))):
                            pe.matmul(PS[2 * gate_at + par][:, u * B:(u + 1) * B], wr["V" + gate][:],
                                      cols(HS, j, STEPS * B, u * B, B), start=False, stop=True,
                                      skip_group_check=True).then_inc(sem, 1)
                        if prefetch and u < 6:
                            inputs(j + 1, 1 - par, u // 2, u % 2)
                pe.wait_ge(s.w, 9 * 16)
                for gate_at in range(3):
                    for part in range(2):
                        inputs(0, 0, gate_at, part)
                turn(0, 0, True)
                turn(1, 1, True)
                with pe.Fori(1, NT // 2 - 1) as pair:
                    turn(2 * pair, 0, True)
                    turn(2 * pair + 1, 1, True)
                turn(NT - 2, 0, True)
                turn(NT - 1, 1, False)

            @block.scalar
            def _(act):
                def turn(j, par):
                    for u in range(STEPS):
                        step, sp_ = j * STEPS + u, u % 2
                        for at, (gate, made, done, f) in enumerate((("i", s.i, s.it, ACT.Sigmoid), ("c", s.g, s.gt, ACT.Tanh),
                                                                    ("o", s.o, s.ot, ACT.Sigmoid))):
                            act.wait_ge(made, step + 1)
                            act.activation(gates[:, at, sp_, :], PS[2 * at + par][:, u * B:(u + 1) * B], f,
                                           bias=wr["b" + gate][:]).then_inc(done, 1)
                        act.wait_ge(s.c, step + 1)
                        act.activation(tanhc[:, sp_, :], cell[:, sp_, :], ACT.Tanh).then_inc(s.ct, 1)
                act.wait_ge(s.w, 9 * 16)
                with act.Fori(0, NT // 2) as pair:
                    turn(2 * pair, 0)
                    turn(2 * pair + 1, 1)

            @block.vector
            def _(v):
                def turn(j, par):
                    for u in range(STEPS):
                        step, q = j * STEPS + u, u % 2
                        if not (isinstance(j, int) and step == 0):
                            v.wait_ge(s.h, step)
                        v.tensor_tensor(hc[:, q, :], cols(HS, j, STEPS * B, u * B, B), cell[:, 1 - q, :],
                                        ALU.mult).then_inc(s.hc, 1)
                        v.wait_ge(s.gt, step + 1)
                        v.wait_ge(s.it, step + 1)
                        v.tensor_tensor(ig[:, q, :], gates[:, 0, q, :], gates[:, 1, q, :], ALU.mult).then_inc(s.ig, 1)
                        v.wait_ge(s.hc, step + 1)
                        v.wait_ge(s.ig, step + 1)
                        v.tensor_tensor(cell[:, q, :], hc[:, q, :], ig[:, q, :], ALU.add).then_inc(s.c, 1)
                        v.wait_ge(s.ot, step + 1)
                        v.wait_ge(s.ct, step + 1)
                        v.tensor_tensor(cols(HS, j, STEPS * B, (u + 1) * B, B), gates[:, 2, q, :], tanhc[:, q, :],
                                        ALU.mult).then_inc(s.h, 1)
                v.wait_ge(s.zero, 2)
                turn(0, 0)
                turn(1, 1)
                with v.Fori(1, NT // 2) as pair:
                    turn(2 * pair, 0)
                    turn(2 * pair + 1, 1)

        layer()
        s = sems("l1", "w in0 in1 sum inv inv2 adjn adjT_ps adjT h h_ps x1 raw mv var rstd xn x_ps xT xw_ps xw conv relu back x2 "
                       "raw2 mv2 var2 rstd2 xn2 y_ps feat")
        wtop = lb("wtop", [H, H])
        wbot = lb("wbot", [H, H])
        b1g = lb("b1g", [H, 1])
        ROWS = lb("ROWS", [P, 2, 2, G])
        XM = lb("XM", [P, B])
        MEAN4 = lb("MEAN4", [P, B])
        RSTD4 = lb("RSTD4", [P, B])
        HS_v = HS[:, B:].rearrange("p (t b) -> p b t", b=B)
        with nc.Block() as block:
            @block.sync
            def _(sp):
                sp.dma_start(wtop[:], a["L1_gnn_weight"][0:H, :]).then_inc(s.w, 16)
                sp.dma_start(wbot[:], a["L1_gnn_weight"][H:2 * H, :]).then_inc(s.w, 16)
                sp.dma_start(b1g[:], column(a["L1_gnn_bias"])).then_inc(s.w, 16)

                def load(i, par, half):
                    reused(sp, s.adjT_ps, i, 2)
                    sp.dma_start(STAGE[:, par].rearrange("p (b j) -> p b j", b=G),
                                 dgroup(adj_v, i)).then_inc((s.in0, s.in1)[par], 16)
                pipelined(sp, NG, [(0, load)])

            @block.gpsimd
            def _(pool):
                def hidden(i, par, half):
                    reused(pool, s.h_ps, i, 2)
                    src = HS_v[:, G * i:G * i + G, :] if isinstance(i, int) else HS_v[:, bass.ds(i * G, G), :]
                    pool.tensor_copy(WF[:, par].rearrange("p (b t) -> p b t", b=G), src).then_inc(s.h, 1)

                def dev(i, par, half):
                    inverse_deviation(pool, i, par, MV, RS, s.mv, s.var, s.rstd)

                def dev2(i, par, half):
                    inverse_deviation(pool, i, par, MVB, RSB, s.mv2, s.var2, s.rstd2)
                pipelined(pool, NG, [(0, hidden), (1, dev), (3, dev2)])

            @block.vector
            def _(v):
                def rows(i, par, half):
                    v.wait_ge((s.in0, s.in1)[par], 16 * half + 16)
                    v.reduce_sum(ROWS[:, par, 0, :], STAGE[:, par].rearrange("p (b j) -> p b j", b=G), AX.X).then_inc(s.sum, 1)
                    v.wait_ge(s.sum, i + 1)
                    v.tensor_scalar(ROWS[:, par, 1, :], ROWS[:, par, 0, :], DENOM_EPS, None, ALU.add).then_inc(s.inv, 1)
                    v.wait_ge(s.inv, i + 1)
                    v.reciprocal(ROWS[:, par, 0, :], ROWS[:, par, 1, :]).then_inc(s.inv2, 1)
                    v.wait_ge(s.inv2, i + 1)
                    for k in range(G):
                        last = v.tensor_scalar(tile(STAGE[:, par], k), tile(STAGE[:, par], k), ROWS[:, par, 0, k:k + 1],
                                               None, ALU.mult)
                    last.then_inc(s.adjn, 1)

                def add(i, par, half):
                    v.wait_ge(s.h_ps, i + 1)
                    v.tensor_tensor(cols(X, i), cols(X, i), PS[0], ALU.add).then_inc(s.x1, 1)
                    wait_apart(v, s.x1, i + 1)
                    statistics(v, i, par, STATS, MV, s.raw, s.mv)

                def norm(i, par, half):
                    v.wait_ge(s.rstd, i + 1)
                    reused(v, s.x_ps, i, 2)
                    normalise(v, i, par, WA, MV, RS, 1, s.xn)

                def add2(i, par, half):
                    v.wait_ge(s.back, i + 1)
                    v.tensor_tensor(cols(X, i), cols(X, i), PS[5], ALU.add).then_inc(s.x2, 1)
                    wait_apart(v, s.x2, i + 1)
                    statistics(v, i, par, STATSB, MVB, s.raw2, s.mv2)

                def norm2(i, par, half):
                    v.wait_ge(s.rstd2, i + 1)
                    reused(v, s.y_ps, i, 2)
                    normalise(v, i, par, WE, MVB, RSB, 1, s.xn2)
                    v.tensor_copy(cols(MEAN4, i, G), MVB[:, par, :, 0])
                    v.tensor_copy(cols(RSTD4, i, G), RSB[:, par, 1, :])
                pipelined(v, NG, [(4, norm2), (2, norm), (1, add), (3, add2), (1, rows)])

            @block.tensor
            def _(pe):
                def hidden(i, par, half):
                    pe.wait_ge(s.h, i + 1)
                    reused(pe, s.x1, i, 1)
                    transpose4(pe, PS[0], WF[:, par], s.h_ps)

                def adjT(i, par, half):
                    pe.wait_ge(s.adjn, i + 1)
                    reused(pe, s.adjT, i, 1)
                    transpose4(pe, PS[1], STAGE[:, par], s.adjT_ps)

                def xT(i, par, half):
                    pe.wait_ge(s.xn, i + 1)
                    reused(pe, s.xT, i, 1)
                    transpose4(pe, PS[2], WA[:, par], s.x_ps)

                def project(i, par, half):
                    pe.wait_ge(s.xT, i + 1)
                    reused(pe, s.xw, i, 1)
                    for k in range(G):
                        last = pe.matmul(tile(PS[3], k), tile(WB[:, par], k), wbot[:], start=True, stop=True)
                    last.then_inc(s.xw_ps, 1)

                def conv(i, par, half):
                    reused(pe, s.relu, i, 1)
                    pe.matmul(PS[4], wtop[:], WB[:, par], start=True, stop=False, skip_group_check=True)
                    pe.wait_ge(s.xw, i + 1)
                    pe.wait_ge(s.adjT, i + 1)
                    for k in range(G):
                        last = pe.matmul(tile(PS[4], k), tile(WC[:, par], k), tile(WC2[:, par], k),
                                         start=False, stop=True, skip_group_check=True)
                    last.then_inc(s.conv, 1)

                def back(i, par, half):
                    pe.wait_ge(s.relu, i + 1)
                    reused(pe, s.x2, i, 1)
                    transpose4(pe, PS[5], WD[:, par], s.back)

                def feat(i, par, half):
                    pe.wait_ge(s.xn2, i + 1)
                    reused(pe, s.feat, i, 1)
                    transpose4(pe, PS[6], WE[:, par], s.y_ps)
                pe.wait_ge(s.w, 3 * 16)
                pipelined(pe, NG, [(3, conv), (2, xT), (0, hidden), (3, back), (2, adjT), (2, project), (4, feat)])

            @block.scalar
            def _(act):
                def adjT(i, par, half):
                    act.wait_ge(s.adjT_ps, i + 1)
                    reused(act, s.conv, i, 2)
                    act.copy(WC2[:, par], PS[1]).then_inc(s.adjT, 1)

                def xT(i, par, half):
                    act.wait_ge(s.x_ps, i + 1)
                    reused(act, s.conv, i, 2)
                    act.copy(WB[:, par], PS[2]).then_inc(s.xT, 1)

                def xw(i, par, half):
                    act.wait_ge(s.xw_ps, i + 1)
                    reused(act, s.conv, i, 2)
                    act.copy(WC[:, par], PS[3]).then_inc(s.xw, 1)

                def relu(i, par, half):
                    act.wait_ge(s.conv, i + 1)
                    reused(act, s.back, i, 2)
                    act.activation(WD[:, par], PS[4], ACT.Relu, bias=b1g[:]).then_inc(s.relu, 1)

                def feat(i, par, half):
                    act.wait_ge(s.y_ps, i + 1)
                    for k in range(G):
                        last = act.activation(cols(FEAT, i, GW, k * T, T), tile(PS[6], k), ACT.Copy,
                                              accum_out=cols(XM, i, G, k, 1))
                    last.then_inc(s.feat, 1)
                act.wait_ge(s.w, 3 * 16)
                pipelined(act, NG, [(3, relu), (2, xT), (2, adjT), (2, xw), (4, feat)])

        s = sems("route", "w br lg m nm e sm rs rw ld l1 l2 scl sc m2 nm2 e2 sm2 rs2 rw2 top idx d ed den w1 w2 idf "
                          "eq diag diag2 bc wb ib ibi wd1 wd2 wd wdT wdTs bm bms row iota scratch rows")
        wr1 = lb("wr1", [H, E1])
        br1 = lb("br1", [B, E1])
        b2_1 = lb("b2_1", [E1, H])
        R = lb("R", [B, 18, E1])
        c1 = lb("c1", [B, 6])
        IDXU = lb("IDXU", [B, 8], UINT32)
        IDXF = lb("IDXF", [B, 8])
        DIAG = lb("DIAG", [B, 2, B, 2])
        WBC = lb("WBC", [P, B * 2])
        EIDX = lb("EIDX", [1, B * 2], INT32)
        WDT = lb("WDT", [E1, B])
        B2M = lb("B2M", [B, H])
        scratch = nc.dram_tensor("scratch_b2", (B, H), FP32, kind="Internal").ap()
        W1_1 = EXP[:, 0:E1 * F1].rearrange("p (e f) -> p e f", e=E1)
        W2_1 = EXP[:, E1 * F1:2 * E1 * F1].rearrange("p (c d) -> p c d", d=H)
        b1_1 = lb("b1_1", [P, E1 * C1])
        gam = lb("gam", [P, H])
        bet = lb("bet", [P, H])
        load_e1 = ctx.enter_context(nc.semaphore("load_e1"))
        with nc.Block() as block:
            @block.sync
            def _(sp):
                sp.dma_start(wr1[:], a["L1_ffn_Wr"]).then_inc(s.w, 16)
                sp.dma_start(br1[:], a["L1_ffn_br"].partition_broadcast(B)).then_inc(s.w, 16)
                sp.dma_start(b2_1[:], a["L1_ffn_b2"]).then_inc(s.w, 16)
                sp.dma_start(W1_1, a["L1_ffn_W1"].rearrange("e d f -> d e f")).then_inc(load_e1, 16)
                sp.dma_start(W2_1, a["L1_ffn_W2"].rearrange("e (c p) d -> p (e c) d", p=P)).then_inc(load_e1, 16)
                sp.dma_start(b1_1[:], a["L1_ffn_b1_T"]).then_inc(load_e1, 16)
                sp.dma_start(gam[:], a["L1_ffn_gamma"].partition_broadcast(P)).then_inc(load_e1, 16)
                sp.dma_start(bet[:], a["L1_ffn_beta"].partition_broadcast(P)).then_inc(load_e1, 16)
                sp.wait_ge(s.bms, 1)
                sp.dma_start(scratch, B2M[:]).then_inc(s.scratch, 16)
                sp.wait_ge(s.scratch, 16)

            @block.tensor
            def _(pe):
                pe.wait_ge(s.w, 3 * 16)
                pe.matmul(PS[0][0:B, 0:E1], XM[:], wr1[:], start=True, stop=True).then_inc(s.lg, 1)
                pe.wait_ge(s.rw, 1)
                pe.matmul(PS[1][0:B, 0:E1], ones[0:B, 0:B], R[:, 4, :], start=True, stop=True).then_inc(s.ld, 1)
                pe.wait_ge(s.wd, 1)
                pe.transpose(PS[2][0:E1, 0:B], R[:, 14, :], ident[0:B, 0:B]).then_inc(s.wdT, 1)
                pe.wait_ge(s.diag2, 1)
                pe.matmul(PS[3][:, 0:4 * B], ones[0:B, :], DIAG[:].rearrange("p a b k -> p (a b k)"),
                          start=True, stop=True).then_inc(s.bc, 1)
                pe.wait_ge(s.wdTs, 1)
                pe.matmul(PS[4][0:B, 0:H], WDT[:], b2_1[:], start=True, stop=True).then_inc(s.bm, 1)

            @block.scalar
            def _(act):
                act.wait_ge(s.nm, 1)
                act.activation(R[:, 2, :], R[:, 0, :], ACT.Exp, bias=c1[:, 0:1], accum_out=c1[:, 1:2]).then_inc(s.e, 1)
                act.wait_ge(s.nm2, 1)
                act.activation(R[:, 8, :], R[:, 6, :], ACT.Exp, bias=c1[:, 2:3], accum_out=c1[:, 3:4]).then_inc(s.e2, 1)
                act.wait_ge(s.d, 1)
                act.activation(R[:, 11, 1:2], R[:, 11, 0:1], ACT.Exp).then_inc(s.ed, 1)

            @block.vector
            def _(v):
                v.wait_ge(s.w, 3 * 16)
                v.wait_ge(s.lg, 1)
                v.scalar_tensor_tensor(R[:, 0, :], PS[0][0:B, 0:E1], 1.0 / T, br1[:], ALU.mult, ALU.add).then_inc(s.m, 1)
                v.wait_ge(s.m, 1)
                v.tensor_reduce(c1[:, 0:1], R[:, 0, :], AX.X, ALU.max, negate=True).then_inc(s.nm, 1)
                v.wait_ge(s.e, 1)
                v.reciprocal(R[:, 3, 0:1], c1[:, 1:2]).then_inc(s.rs, 1)
                v.wait_ge(s.rs, 1)
                v.tensor_scalar(R[:, 4, :], R[:, 2, :], R[:, 3, 0:1], None, ALU.mult).then_inc(s.rw, 1)
                v.wait_ge(s.ld, 1)
                v.tensor_scalar(R[:, 5, :], PS[1][0:B, 0:E1], float(T), None, ALU.mult).then_inc(s.l1, 1)
                v.wait_ge(s.l1, 1)
                v.reciprocal(R[:, 7, :], R[:, 5, :]).then_inc(s.l2, 1)
                v.wait_ge(s.l2, 1)
                v.tensor_scalar(R[:, 9, :], R[:, 7, :], CAPACITY, 1.0, ALU.mult, ALU.min).then_inc(s.scl, 1)
                v.wait_ge(s.scl, 1)
                v.tensor_tensor(R[:, 6, :], R[:, 4, :], R[:, 9, :], ALU.mult).then_inc(s.sc, 1)
                v.wait_ge(s.sc, 1)
                v.tensor_reduce(c1[:, 2:3], R[:, 6, :], AX.X, ALU.max, negate=True).then_inc(s.nm2, 1)
                v.wait_ge(s.e2, 1)
                v.reciprocal(R[:, 3, 1:2], c1[:, 3:4]).then_inc(s.rs2, 1)
                v.wait_ge(s.rs2, 1)
                v.tensor_scalar(R[:, 10, :], R[:, 8, :], R[:, 3, 1:2], None, ALU.mult).then_inc(s.rw2, 1)
                v.wait_ge(s.rw2, 1)
                v.max(R[:, 12, :], R[:, 10, :]).then_inc(s.top, 1)
                v.wait_ge(s.top, 1)
                v.max_index(IDXU[:], R[:, 12, :], R[:, 10, :]).then_inc(s.idx, 1)
                v.tensor_tensor(R[:, 11, 0:1], R[:, 12, 1:2], R[:, 12, 0:1], ALU.subtract).then_inc(s.d, 1)
                v.wait_ge(s.idx, 1)
                v.tensor_copy(IDXF[:], IDXU[:]).then_inc(s.idf, 1)
                v.wait_ge(s.ed, 1)
                v.tensor_scalar(R[:, 11, 2:3], R[:, 11, 1:2], 1.0, None, ALU.add).then_inc(s.den, 1)
                v.wait_ge(s.den, 1)
                v.reciprocal(R[:, 13, 0:1], R[:, 11, 2:3]).then_inc(s.w1, 1)
                v.wait_ge(s.w1, 1)
                v.tensor_tensor(R[:, 13, 1:2], R[:, 13, 0:1], R[:, 11, 1:2], ALU.mult).then_inc(s.w2, 1)
                v.wait_ge(s.w2, 1)
                v.wait_ge(s.idf, 1)
                v.tensor_scalar(R[:, 15, :], iota8[0:B, :], IDXF[:, 0:1], R[:, 13, 0:1], ALU.is_equal, ALU.mult).then_inc(s.wd1, 1)
                v.tensor_scalar(R[:, 16, :], iota8[0:B, :], IDXF[:, 1:2], R[:, 13, 1:2], ALU.is_equal, ALU.mult).then_inc(s.wd2, 1)
                v.wait_ge(s.wd1, 1)
                v.wait_ge(s.wd2, 1)
                v.tensor_tensor(R[:, 14, :], R[:, 15, :], R[:, 16, :], ALU.add).then_inc(s.wd, 1)
                for k in range(2):
                    v.tensor_scalar(DIAG[:, 0, :, k], ident[0:B, 0:B], R[:, 13, k:k + 1], None, ALU.mult).then_inc(s.diag, 1)
                    last = v.tensor_scalar(DIAG[:, 1, :, k], ident[0:B, 0:B], IDXF[:, k:k + 1], None, ALU.mult)
                last.then_inc(s.diag2, 1)
                v.wait_ge(s.wdT, 1)
                v.tensor_copy(WDT[:], PS[2][0:E1, 0:B]).then_inc(s.wdTs, 1)
                v.wait_ge(s.bc, 1)
                v.tensor_copy(WBC[:], PS[3][:, 0:2 * B]).then_inc(s.wb, 1)
                v.tensor_copy(EIDX[:], PS[3][0:1, 2 * B:4 * B]).then_inc(s.ib, 1)
                v.wait_ge(s.bm, 1)
                v.tensor_copy(B2M[:], PS[4][0:B, 0:H]).then_inc(s.bms, 1)

        s = sems("ex1", "rows0 rows1 w1 w2 h_ps gelu y_ps xn xb z raw mv var rstd n1 n2 n3 x1")
        W1S = EXP[:, 2 * E1 * F1:2 * E1 * F1 + 4 * F1].rearrange("p (a f) -> p a f", a=2)
        W2S = EXP[:, 2 * E1 * F1 + 4 * F1:2 * E1 * F1 + 8 * F1].rearrange("p (a f) -> p a f", a=2)
        B1S = lb("B1S", [P, 2, 2 * C1])
        HB = WF
        B2R = STAGE
        XN1, XB1, Z1, ZN1, ZM1, ZO1 = (WA, WB, WC, WD, WE, WC2)
        row_v = scratch.rearrange("(g b) h -> g (b h)", b=G)
        with nc.Block() as block:
            @block.sync
            def _(sp):
                def rows(i, par, half):
                    reused(sp, s.xb, i, 2)
                    src = scratch[i:i + 1, :] if isinstance(i, int) else scratch[bass.ds(i, 1), :]
                    sp.dma_start(B2R[:, par, 0:H], src.rearrange("o h -> (o h)").partition_broadcast(P)).then_inc(
                        (s.rows0, s.rows1)[par], 16)
                pipelined(sp, B, [(0, rows)])

            @block.gpsimd
            def _(pool):
                def first(i, par, half):
                    reused(pool, s.gelu, i, 2)
                    for k in range(2):
                        e = pool.value_load(cols(EIDX, i, 2, k, 1), min_val=0, max_val=E1 - 1)
                        pool.tensor_copy(W1S[:, par, k * F1:(k + 1) * F1],
                                         W1_1[:, bass.ds(e, 1), :].rearrange("p a f -> p (a f)"))
                        last = pool.tensor_copy(B1S[:, par, k * C1:(k + 1) * C1], b1_1[:, bass.ds(e * C1, C1)])
                    last.then_inc(s.w1, 1)

                def bias(i, par, half):
                    pool.wait_ge(s.xn, i + 1)
                    pool.wait_ge((s.rows0, s.rows1)[par], 16 * half + 16)
                    reused(pool, s.z, i, 2)
                    pool.tensor_tensor(XB1[:, par, 0:H], XN1[:, par, 0:H], B2R[:, par, 0:H], ALU.add).then_inc(s.xb, 1)

                def dev(i, par, half):
                    pool.wait_ge(s.mv, i + 1)
                    pool.tensor_tensor(RSB[:, par, 0, 0:1], MVB[:, par, 0, 1:2], epsilon[:, 0:1], ALU.add).then_inc(s.var, 1)
                    pool.wait_ge(s.var, i + 1)
                    pool.tensor_tensor(RSB[:, par, 1, 0:1], RSB[:, par, 0, 0:1], mhalf[:, 0:1], ALU.pow).then_inc(s.rstd, 1)

                def gamma(i, par, half):
                    pool.wait_ge(s.n1, i + 1)
                    pool.tensor_tensor(ZM1[:, par, 0:H], ZN1[:, par, 0:H], gam[:], ALU.mult).then_inc(s.n2, 1)
                    pool.wait_ge(s.n2, i + 1)
                    reused(pool, s.x1, i, 2)
                    pool.tensor_tensor(ZO1[:, par, 0:H], ZM1[:, par, 0:H], bet[:], ALU.add).then_inc(s.n3, 1)
                pool.wait_ge(load_e1, 5 * 16)
                pipelined(pool, B, [(0, first), (1, bias), (2, dev), (3, gamma)])

            @block.tensor
            def _(pe):
                def up(i, par, half):
                    pe.wait_ge(s.w1, i + 1)
                    reused(pe, s.gelu, i, 2)
                    for k in range(2 * C1):
                        last = pe.matmul(tile(PS[par], k), W1S[:, par, k * P:(k + 1) * P], cols(FEAT, i, T),
                                         start=True, stop=True)
                    last.then_inc(s.h_ps, 1)

                def down(i, par, half):
                    pe.wait_ge(s.gelu, i + 1)
                    pe.wait_ge(s.w2, i + 1)
                    reused(pe, s.z, i, 2)
                    for k in range(2 * C1):
                        last = pe.matmul(PS[2 + par][:, 0:H], tile(HB[:, par], k), W2S[:, par, k * H:(k + 1) * H],
                                         start=(k == 0), stop=(k == 2 * C1 - 1))
                    last.then_inc(s.y_ps, 1)
                pipelined(pe, B, [(1, up), (2, down)])

            @block.scalar
            def _(act):
                def gelu(i, par, half):
                    act.wait_ge(s.h_ps, i + 1)
                    reused(act, s.y_ps, i, 2)
                    for k in range(2 * C1):
                        last = act.activation(tile(HB[:, par], k), tile(PS[par], k), ACT.Gelu, bias=B1S[:, par, k:k + 1])
                    last.then_inc(s.gelu, 1)
                pipelined(act, B, [(1, gelu)])

            @block.vector
            def _(v):


                def second(i, par, half):
                    reused(v, s.y_ps, i, 2)
                    for k in range(2):
                        e = v.value_load(cols(EIDX, i, 2, k, 1), min_val=0, max_val=E1 - 1)
                        last = v.tensor_scalar(W2S[:, par, k * F1:(k + 1) * F1],
                                               W2_1.rearrange("p c d -> p (c d)")[:, bass.ds(e * F1, F1)],
                                               cols(WBC, i, 2, k, 1), None, ALU.mult)
                    last.then_inc(s.w2, 1)

                def norm(i, par, half):
                    reused(v, s.xb, i, 2)
                    v.tensor_scalar(XN1[:, par, 0:H], cols(X, i, H), cols(MEAN4, i, 1), cols(RSTD4, i, 1),
                                    ALU.subtract, ALU.mult).then_inc(s.xn, 1)

                def add(i, par, half):
                    v.wait_ge(s.y_ps, i + 1)
                    v.wait_ge(s.xb, i + 1)
                    v.tensor_tensor(Z1[:, par, 0:H], PS[2 + par][:, 0:H], XB1[:, par, 0:H], ALU.add).then_inc(s.z, 1)
                    v.wait_ge(s.z, i + 1)
                    v.bn_stats(STATSB[:, par, 0, :], Z1[:, par, 0:H]).then_inc(s.raw, 1)
                    wait_apart(v, s.raw, i + 1)
                    v.bn_aggr(MVB[:, par, 0, :], STATSB[:, par, 0, :]).then_inc(s.mv, 1)

                def norm2(i, par, half):
                    v.wait_ge(s.rstd, i + 1)
                    reused(v, s.n2, i, 2)
                    v.tensor_scalar(ZN1[:, par, 0:H], Z1[:, par, 0:H], MVB[:, par, 0, 0:1], RSB[:, par, 1, 0:1],
                                    ALU.subtract, ALU.mult).then_inc(s.n1, 1)

                def residual(i, par, half):
                    v.wait_ge(s.n3, i + 1)
                    v.tensor_tensor(cols(X, i, H), cols(X, i, H), ZO1[:, par, 0:H], ALU.add).then_inc(s.x1, 1)
                v.wait_ge(load_e1, 5 * 16)
                pipelined(v, B, [(1, norm), (3, norm2), (4, residual), (1, second), (2, add)])

        layer()
        s = sems("l2a", "w zero raw mv var rstd xn x_ps xT keep v_ps v x1 scaled")
        WqP = lb("WqP", [P, HEADS, HP])
        WkP = lb("WkP", [P, HEADS, HP])
        WvT = lb("WvT", [P, H])
        WoP = lb("WoP", [P, NC, H])
        bo_b = lb("bo_b", [P, H])
        VAL = AUX
        with nc.Block() as block:
            @block.sync
            def _(sp):
                sp.wait_ge(s.zero, 3)
                heads = lambda v: v.rearrange("i (h d) -> i h d", h=HEADS)
                sp.dma_start(WqP[:, :, 0:HD], heads(a["L2_gnn_Wq_T"])).then_inc(s.w, 16)
                sp.dma_start(WkP[:, :, 0:HD], heads(a["L2_gnn_Wk_T"])).then_inc(s.w, 16)
                sp.dma_start(WvT[:], a["L2_gnn_Wv_T"]).then_inc(s.w, 16)
                sp.dma_start(bo_b[:], a["L2_gnn_bo"].partition_broadcast(P)).then_inc(s.w, 16)
                for chunk in range(NC):
                    for tile_at in range(HC):
                        h = HC * (tile_at % 2) + 2 * chunk + tile_at // 2
                        sp.dma_start(WoP[HP * tile_at:HP * tile_at + HD, chunk, :],
                                     a["L2_gnn_Wo_T"][h * HD:(h + 1) * HD, :]).then_inc(s.w, 16)

            @block.gpsimd
            def _(pool):
                pool.memset(WqP[:], 0.0).then_inc(s.zero, 1)
                pool.memset(WkP[:], 0.0).then_inc(s.zero, 1)
                pool.memset(WoP[:], 0.0).then_inc(s.zero, 1)

                def dev(i, par, half):
                    inverse_deviation(pool, i, par, MV, RS, s.mv, s.var, s.rstd)

                def keep(i, par, half):
                    pool.wait_ge(s.xT, i + 1)
                    pool.tensor_copy(cols(FEAT, i), WB[:, par]).then_inc(s.keep, 1)
                    pool.wait_ge(s.xn, i + 1)
                    x = cols(X, i).rearrange("p (b h) -> p b h", b=G)
                    pool.tensor_tensor(x, x, bo_b[:].unsqueeze(1).to_broadcast([P, G, H]), ALU.add).then_inc(s.x1, 1)
                pool.wait_ge(s.w, 12 * 16)
                pipelined(pool, NG, [(0, dev), (2, keep)])

            @block.vector
            def _(v):
                def stats(i, par, half):
                    statistics(v, i, par, STATS, MV, s.raw, s.mv)

                def norm(i, par, half):
                    v.wait_ge(s.rstd, i + 1)
                    reused(v, s.x_ps, i, 2)
                    normalise(v, i, par, WA, MV, RS, 1, s.xn)
                v.wait_ge(s.w, 12 * 16)
                v.tensor_scalar(WqP[:], WqP[:], float(HD) ** -0.5, None, ALU.mult).then_inc(s.scaled, 1)
                pipelined(v, NG, [(1, norm), (0, stats)])

            @block.tensor
            def _(pe):
                def xT(i, par, half):
                    pe.wait_ge(s.xn, i + 1)
                    reused(pe, s.xT, i, 1)
                    transpose4(pe, PS[0], WA[:, par], s.x_ps)

                def values(i, par, half):
                    pe.wait_ge(s.xT, i + 1)
                    reused(pe, s.v, i, 1)
                    for k in range(G):
                        last = pe.matmul(tile(PS[1], k), tile(WB[:, par], k), WvT[:], start=True, stop=True)
                    last.then_inc(s.v_ps, 1)
                pe.wait_ge(s.w, 12 * 16)
                pipelined(pe, NG, [(2, values), (1, xT)])

            @block.scalar
            def _(act):
                def xT(i, par, half):
                    act.wait_ge(s.x_ps, i + 1)
                    reused(act, s.keep, i, 2)
                    reused(act, s.v_ps, i, 2)
                    act.copy(WB[:, par], PS[0]).then_inc(s.xT, 1)

                def values(i, par, half):
                    act.wait_ge(s.v_ps, i + 1)
                    act.copy(cols(VAL, i), PS[1]).then_inc(s.v, 1)
                pipelined(act, NG, [(2, values), (1, xT)])

        s = sems("att", "zero qk_ps qk score top ex pT pTa vp pv inv ot y x1")
        SW = HEADS * T
        EXS = EXP[:, 0:2 * SW].rearrange("p (a n) -> p a n", a=2)
        PTA = EXP[:, 2 * SW:4 * SW].rearrange("p (a n) -> p a n", a=2)
        QKS = WA
        OT, INV = WC, WD
        VP = EXP[:, 4 * SW:4 * SW + 2 * HEADS * HP].rearrange("p (a h d) -> p a h d", a=2, h=HEADS)
        NEGMAX = lb("NEGMAX", [P, 2, HEADS])
        with nc.Block() as block:
            @block.gpsimd
            def _(pool):
                pool.memset(VP, 0.0).then_inc(s.zero, 1)
                pool.wait_ge(s.zero, 1)

                def vp(i, par, half):
                    reused(pool, s.pv, i, 2)
                    pool.tensor_copy(VP[:, par, :, 0:HD], cols(VAL, i, H).rearrange("p (h d) -> p h d", h=HEADS)
                                     ).then_inc(s.vp, 1)
                pipelined(pool, B, [(1, vp)])

            @block.tensor
            def _(pe):
                def qk(i, par, half):
                    reused(pe, s.qk, i, 1)
                    for at, wt in enumerate((WqP, WkP)):
                        for c in range(NC):
                            last = pe.matmul(tile(PS[6], at * NC + c), wt[:, c * HC:(c + 1) * HC, :].rearrange("p h d -> p (h d)"),
                                             cols(FEAT, i, T), start=True, stop=True)
                    last.then_inc(s.qk_ps, 1)

                def scores(i, par, half):
                    pe.wait_ge(s.qk, i + 1)
                    reused(pe, s.ex, i, 1, 2)
                    for j in range(HC):
                        rows = slice(HP * j, HP * (j + 1))
                        for c in range(NC):
                            last = pe.matmul(tile(PS[j], c), QKS[rows, par, c * T:(c + 1) * T],
                                             QKS[rows, par, (NC + c) * T:(NC + c + 1) * T], start=True, stop=True)
                        if j % 2:
                            last.then_inc(s.score, 1)

                def transpose(i, par, half):
                    for k in range(2):
                        if not isinstance(i, int) or i >= 1:
                            pe.wait_ge(s.pTa, 2 * i)
                            if not isinstance(i, int) or i >= 2:
                                pe.wait_ge(s.x1, i - 1)
                        pe.wait_ge(s.ex, 2 * i + k + 1)
                        for n in range(4):
                            last = pe.transpose(tile(PS[4 + k], n), tile(EXS[:, par], 4 * k + n), ident[:])
                        last.then_inc(s.pT, 1)

                def product(i, par, half):
                    pe.wait_ge(s.vp, i + 1)
                    reused(pe, s.ot, i, 1)
                    for k in range(NC):
                        pe.wait_ge(s.pTa, 2 * i + k + 1)
                        for what in range(2):
                            for n in range(HC):
                                h = HC * (n % 2) + 2 * k + n // 2
                                lhsT = ones[:, 0:HP] if what else VP[:, par, h, :]
                                at = (2 * what + k) * T
                                last = pe.matmul(PS[7][HP * n:HP * (n + 1), at:at + T], lhsT,
                                                 tile(PTA[:, par], 4 * k + n), start=True, stop=True)
                    last.then_inc(s.pv, 1)

                def output(i, par, half):
                    pe.wait_ge(s.ot, i + 1)
                    pe.wait_ge(s.pTa, min(2 * i + 3, 2 * B) if isinstance(i, int) else 2 * i + 3)
                    if isinstance(i, int) and i == B - 1:
                        pe.wait_ge(s.x1, i)
                    for k in range(NC):
                        last = pe.matmul(PS[4][:, 0:H], OT[:, par, k * T:(k + 1) * T], WoP[:, k, :],
                                         start=(k == 0), stop=(k == NC - 1))
                    last.then_inc(s.y, 1)
                pipelined(pe, B, [(1, scores), (2, transpose), (0, qk), (2, product), (3, output)])

            @block.scalar
            def _(act):
                def qk(i, par, half):
                    act.wait_ge(s.qk_ps, i + 1)
                    reused(act, s.score, i, 2, 2)
                    act.copy(QKS[:, par], PS[6]).then_inc(s.qk, 1)

                def exps(i, par, half):
                    reused(act, s.pT, i, 2, 2)
                    for k in range(2):
                        act.wait_ge(s.top, 2 * i + k + 1)
                        for n in range(4):
                            j, c = 2 * k + n // 2, n % 2
                            last = act.activation(tile(EXS[:, par], 4 * k + n), tile(PS[j], c), ACT.Exp,
                                                  bias=NEGMAX[:, par, 4 * k + n:4 * k + n + 1])
                        last.then_inc(s.ex, 1)
                pipelined(act, B, [(1, exps), (0, qk)])

            @block.vector
            def _(v):
                def tops(i, par, half):
                    reused(v, s.ex, i, 2, 2)
                    for k in range(2):
                        v.wait_ge(s.score, 2 * i + k + 1)
                        v.tensor_reduce(NEGMAX[:, par, 4 * k:4 * k + 4].rearrange("p (j c) -> p j c", j=2),
                                        BANKS[:, 2 * k:2 * k + 2, 0:NC * T].rearrange("p j (c t) -> p j c t", c=NC),
                                        AX.X, ALU.max, negate=True).then_inc(s.top, 1)

                def weigh(i, par, half):
                    reused(v, s.pv, i, 2)
                    for k in range(2):
                        v.wait_ge(s.pT, 2 * i + k + 1)
                        adj = cols(AT, i, T).unsqueeze(1).to_broadcast([P, 4, T])
                        v.scalar_tensor_tensor(PTA[:, par, 4 * k * T:4 * (k + 1) * T].rearrange("p (n t) -> p n t", n=4),
                                               adj, ADJ_EPS, PS[4 + k].rearrange("p (n t) -> p n t", n=4),
                                               ALU.add, ALU.mult).then_inc(s.pTa, 1)

                def divide(i, par, half):
                    v.wait_ge(s.pv, i + 1)
                    v.reciprocal(INV[:, par, 0:NC * T], PS[7][:, NC * T:2 * NC * T]).then_inc(s.inv, 1)
                    v.wait_ge(s.inv, i + 1)
                    reused(v, s.y, i, 2)
                    v.tensor_tensor(OT[:, par, 0:NC * T], PS[7][:, 0:NC * T], INV[:, par, 0:NC * T], ALU.mult).then_inc(s.ot, 1)

                def add(i, par, half):
                    v.wait_ge(s.y, i + 1)
                    v.tensor_tensor(cols(X, i, H), cols(X, i, H), PS[4][:, 0:H], ALU.add).then_inc(s.x1, 1)
                pipelined(v, B, [(1, tops), (2, weigh), (2, divide), (3, add)])

        layer()
        s = sems("rt2", "w one raw mv var rstd xn x_ps xT keep lg_ps lg top idx idf d th w2 w1 m1 mask")
        NE = E2 + 1
        wr2 = lb("wr2", [H, E2])
        MASK = lb("MASK", [P, B, NE])
        LG = lb("LG", [P, 2, G, E2])
        TOP = lb("TOP", [P, 2, G, 8])
        IDX = lb("IDX", [P, 2, G, 8], UINT32)
        IDXG = lb("IDXG", [P, 2, G, 8])
        TH = lb("TH", [P, 2, 4, G])
        M1 = lb("M1", [P, 2, 2, G, E2])
        b1_2 = lb("b1_2", [P, NE * C2])
        b2_2 = lb("b2_2", [NE, H])
        W1_2 = AUX[:, 0:E2 * F2].rearrange("p (e f) -> p e f", e=E2)
        W2_2 = AUX[:, E2 * F2:2 * E2 * F2].rearrange("p (c d) -> p c d", d=H)
        W1_sh, W2_sh = WC[:, 0], WC[:, 1].rearrange("p (c d) -> p c d", d=H)
        load_e2 = ctx.enter_context(nc.semaphore("load_e2"))
        with nc.Block() as block:
            @block.sync
            def _(sp):
                sp.dma_start(wr2[:], a["L2_ffn_Wr"]).then_inc(s.w, 16)
                sp.dma_start(W1_sh, a["L2_ffn_W1s"]).then_inc(load_e2, 16)
                sp.dma_start(W2_sh, a["L2_ffn_W2s"].rearrange("(c p) d -> p c d", p=P)).then_inc(load_e2, 16)
                sp.dma_start(W1_2, a["L2_ffn_W1p"].rearrange("e d f -> d e f")).then_inc(load_e2, 16)
                sp.dma_start(W2_2, a["L2_ffn_W2p"].rearrange("e (c p) d -> p (e c) d", p=P)).then_inc(load_e2, 16)
                sp.dma_start(b1_2[:, 0:E2 * C2], a["L2_ffn_b1p_T"]).then_inc(load_e2, 16)
                sp.dma_start(b1_2[:, E2 * C2:], a["L2_ffn_b1s_T"]).then_inc(load_e2, 16)
                sp.dma_start(b2_2[0:E2, :], a["L2_ffn_b2p"]).then_inc(load_e2, 16)
                sp.dma_start(b2_2[E2:NE, :], a["L2_ffn_b2s"].rearrange("(o h) -> o h", o=1)).then_inc(load_e2, 16)

            @block.gpsimd
            def _(pool):
                pool.memset(MASK[:, :, E2:NE], 1.0).then_inc(s.one, 1)

                def dev(i, par, half):
                    inverse_deviation(pool, i, par, MV, RS, s.mv, s.var, s.rstd)

                def keep(i, par, half):
                    pool.wait_ge(s.xT, i + 1)
                    pool.tensor_copy(cols(FEAT, i), WB[:, par]).then_inc(s.keep, 1)
                pipelined(pool, NG, [(0, dev), (2, keep)])

            @block.tensor
            def _(pe):
                def xT(i, par, half):
                    pe.wait_ge(s.xn, i + 1)
                    reused(pe, s.xT, i, 1)
                    transpose4(pe, PS[0], WA[:, par], s.x_ps)

                def logits(i, par, half):
                    pe.wait_ge(s.xT, i + 1)
                    reused(pe, s.lg, i, 1)
                    for k in range(G):
                        last = pe.matmul(PS[1][:, k * E2:(k + 1) * E2], tile(WB[:, par], k), wr2[:], start=True, stop=True)
                    last.then_inc(s.lg_ps, 1)
                pe.wait_ge(s.w, 16)
                pipelined(pe, NG, [(2, logits), (1, xT)])

            @block.scalar
            def _(act):
                def xT(i, par, half):
                    act.wait_ge(s.x_ps, i + 1)
                    reused(act, s.keep, i, 2)
                    reused(act, s.lg_ps, i, 2)
                    act.copy(WB[:, par], PS[0]).then_inc(s.xT, 1)

                def th(i, par, half):
                    act.wait_ge(s.d, i + 1)
                    act.activation(TH[:, par, 1, :], TH[:, par, 0, :], ACT.Tanh, scale=0.5).then_inc(s.th, 1)
                pipelined(act, NG, [(3, th), (1, xT)])

            @block.vector
            def _(v):
                def stats(i, par, half):
                    statistics(v, i, par, STATS, MV, s.raw, s.mv)

                def norm(i, par, half):
                    v.wait_ge(s.rstd, i + 1)
                    reused(v, s.x_ps, i, 2)
                    normalise(v, i, par, WA, MV, RS, 1, s.xn)

                def top(i, par, half):
                    v.wait_ge(s.lg_ps, i + 1)
                    v.tensor_copy(LG[:, par].rearrange("p g e -> p (g e)"), PS[1][:, 0:G * E2]).then_inc(s.lg, 1)
                    wait_apart(v, s.lg, i + 1)
                    for k in range(G):
                        last = v.max(TOP[:, par, k, :], LG[:, par, k, :])
                    last.then_inc(s.top, 1)
                    wait_apart(v, s.top, i + 1)
                    for k in range(G):
                        last = v.max_index(IDX[:, par, k, :], TOP[:, par, k, :], LG[:, par, k, :])
                    last.then_inc(s.idx, 1)
                    v.tensor_tensor(TH[:, par, 0, :], TOP[:, par, :, 1], TOP[:, par, :, 0], ALU.subtract).then_inc(s.d, 1)
                    v.wait_ge(s.idx, i + 1)
                    v.tensor_copy(IDXG[:, par], IDX[:, par]).then_inc(s.idf, 1)

                def masks(i, par, half):
                    v.wait_ge(s.th, i + 1)
                    v.tensor_scalar(TH[:, par, 2, :], TH[:, par, 1, :], -0.5, 0.5, ALU.mult, ALU.add).then_inc(s.w1, 1)
                    v.tensor_scalar(TH[:, par, 3, :], TH[:, par, 1, :], 0.5, 0.5, ALU.mult, ALU.add).then_inc(s.w2, 1)
                    v.wait_ge(s.idf, i + 1)
                    v.wait_ge(s.w2, i + 1)
                    for n in range(2):
                        for k in range(G):
                            last = v.tensor_scalar(M1[:, par, n, k, :], iota8[:], IDXG[:, par, k, n:n + 1],
                                                   TH[:, par, 2 + n, k:k + 1], ALU.is_equal, ALU.mult)
                    last.then_inc(s.m1, 1)
                    v.wait_ge(s.m1, i + 1)
                    dst = MASK[:, G * i:G * i + G, 0:E2] if isinstance(i, int) else MASK[:, bass.ds(i * G, G), 0:E2]
                    v.tensor_tensor(dst, M1[:, par, 0], M1[:, par, 1], ALU.add).then_inc(s.mask, 1)
                pipelined(v, NG, [(1, norm), (0, stats), (2, top), (3, masks)])

        s = sems("ex2", "mg mT_ps mT h_ps gelu y acc")
        ORDER = [E2] + list(range(E2))
        HB2 = EXP[:].rearrange("p (a n) -> p a n", a=3)
        MG, MT = WD[:, 0, 0:G * NE], WE[0:NE, 0, 0:GW]
        w1_of = lambda e: W1_sh if e == E2 else W1_2[:, e, :]
        w2_of = lambda e, c: W2_sh[:, c, :] if e == E2 else W2_2[:, e * C2 + c, :]

        def units(eng, part, tail=None):
            for n in range(NE):
                part(0, n, n)
            with eng.Fori(1, NG) as g:
                for n in range(NE):
                    part(g, n, g * NE + n)
            if tail:
                tail()

        with nc.Block() as block:
            @block.gpsimd
            def _(pool):
                def mask(i):
                    reused(pool, s.mT_ps, i, 1)
                    src = cols(MASK[:].rearrange("p b e -> p (b e)"), i, G * NE)
                    pool.tensor_copy(MG, src).then_inc(s.mg, 1)
                mask(0)
                with pool.Fori(1, NG) as i:
                    mask(i)

            @block.tensor
            def _(pe):
                def up(g, n, u):
                    e = ORDER[n]
                    for c in range(C2):
                        if not isinstance(u, int) or u >= 1:
                            pe.wait_ge(s.gelu, (u - 1) * C2 + c + 1)
                        pe.matmul(PS[c], w1_of(e)[:, c * P:(c + 1) * P], cols(FEAT, g), start=True, stop=True
                                  ).then_inc(s.h_ps, 1)

                def down(g, n, u):
                    e = ORDER[n]
                    pe.wait_ge(s.gelu, (u + 1) * C2)
                    reused(pe, s.acc, u, 3)
                    shared = e == E2
                    if shared:
                        pe.wait_ge(s.mT, g + 1)
                    for k in range(G):
                        out_k = tile(PS[4 + n % 3], k)
                        if shared:
                            pe.matmul(out_k, tile(MT, k), b2_2[:], start=True, stop=False)
                        for c in range(C2):
                            last = pe.matmul(out_k, HB2[:, n % 3, c * GW + k * T:c * GW + (k + 1) * T], w2_of(e, c),
                                             start=(c == 0 and not shared), stop=(c == C2 - 1))
                    last.then_inc(s.y, 1)

                def step(g, n, u):
                    if n == 0:
                        pe.wait_ge(s.mg, g + 1)
                        reused(pe, s.mT, g, 1)
                        for k in range(G):
                            last = pe.transpose(PS[7][0:NE, k * T:(k + 1) * T], MG[:, k * NE:(k + 1) * NE], ident[:])
                        last.then_inc(s.mT_ps, 1)
                    up(g, n, u)
                    if n:
                        down(g, n - 1, u - 1)
                    elif not (isinstance(u, int) and u == 0):
                        down(g - 1, NE - 1, u - 1)
                pe.wait_ge(load_e2, 8 * 16)
                units(pe, step, lambda: down(NG - 1, NE - 1, NG * NE - 1))

            @block.scalar
            def _(act):
                def gelu(g, n, u):
                    if n == 0:
                        act.wait_ge(s.mT_ps, g + 1)
                        if not isinstance(g, int):
                            act.wait_ge(s.y, (g - 1) * NE + 1)
                        act.copy(MT, PS[7][0:NE, :]).then_inc(s.mT, 1)
                    e = ORDER[n]
                    reused(act, s.y, u, 3)
                    for c in range(C2):
                        act.wait_ge(s.h_ps, u * C2 + c + 1)
                        act.activation(HB2[:, n % 3, c * GW:(c + 1) * GW], PS[c], ACT.Gelu,
                                       bias=b1_2[:, e * C2 + c:e * C2 + c + 1]).then_inc(s.gelu, 1)
                act.wait_ge(load_e2, 8 * 16)
                units(act, gelu)

            @block.vector
            def _(v):
                def acc(g, n, u):
                    e = ORDER[n]
                    v.wait_ge(s.y, u + 1)
                    reused(v, s.acc, u, 1)
                    if e == E2:
                        last = v.tensor_tensor(cols(X, g), cols(X, g), PS[4 + n % 3], ALU.add)
                    else:
                        for k in range(G):
                            x = cols(X, g, GW, k * H, H)
                            m = cols(MASK[:].rearrange("p b e -> p (b e)"), g, G * NE, k * NE + e, 1)
                            last = v.scalar_tensor_tensor(x, tile(PS[4 + n % 3], k), m, x, ALU.mult, ALU.add)
                    last.then_inc(s.acc, 1)
                units(v, acc)

        layer()
        s = sems("l3", "w raw mv var rstd xn x_ps xT sw_ps sw conv relu back x1 raw2 mv2 var2 rstd2 xn2 f_ps f keep "
                       "lg_ps lg top idx idf hot hT_ps hot_T pos neg dw dws g1 g2")
        dw = lb("dw", [H, H])
        dwn = lb("dwn", [H, H])
        w3 = lb("w3", [H, H])
        b3g = lb("b3g", [H, 1])
        rw3 = lb("rw3", [H, E3])
        rb3 = lb("rb3", [P, E3])
        iota32 = lb("iota32", [P, E3])
        LG3 = lb("LG3", [P, 2, G, E3])
        TOP3 = lb("TOP3", [P, 2, G, 8])
        IDX3 = lb("IDX3", [P, 2, G, 8], UINT32)
        IDXG3 = lb("IDXG3", [P, 2, G, 8])
        HOT = lb("HOT", [P, 2, G, E3])
        HOT_T = AUX[0:E3, 0:B * T]
        b2_3 = lb("b2_3", [E3, H])
        NONE = -1e30
        with nc.Block() as block:
            @block.sync
            def _(sp):
                sp.dma_start(w3[:], a["L3_gnn_weight"]).then_inc(s.w, 16)
                sp.dma_start(b3g[:], column(a["L3_gnn_bias"])).then_inc(s.w, 16)
                sp.dma_start(rw3[:], a["L3_ffn_router_w_T"]).then_inc(s.w, 16)
                sp.dma_start(rb3[:], a["L3_ffn_router_b"].partition_broadcast(P)).then_inc(s.w, 16)
                sp.dma_start(b2_3[:], a["L3_ffn_b2"]).then_inc(s.w, 16)

            @block.gpsimd
            def _(pool):
                pool.iota(iota32[:], [[1, E3]], base=0, channel_multiplier=0, allow_small_or_imprecise_dtypes=True
                          ).then_inc(s.g1, 1)

                def dev(i, par, half):
                    inverse_deviation(pool, i, par, MV, RS, s.mv, s.var, s.rstd)

                def dev2(i, par, half):
                    inverse_deviation(pool, i, par, MVB, RSB, s.mv2, s.var2, s.rstd2)

                def keep(i, par, half):
                    pool.wait_ge(s.f, i + 1)
                    pool.tensor_copy(cols(FEAT, i), WF[:, par]).then_inc(s.keep, 1)
                pipelined(pool, NG, [(0, dev), (2, dev2), (4, keep)])

            @block.tensor
            def _(pe):
                def xT(i, par, half):
                    pe.wait_ge(s.xn, i + 1)
                    reused(pe, s.xT, i, 1)
                    transpose4(pe, PS[0], WA[:, par], s.x_ps)

                def support(i, par, half):
                    pe.wait_ge(s.xT, i + 1)
                    reused(pe, s.sw, i, 1)
                    for k in range(G):
                        last = pe.matmul(tile(PS[1], k), tile(WB[:, par], k), dw[:], start=True, stop=True)
                    last.then_inc(s.sw_ps, 1)

                def conv(i, par, half):
                    pe.wait_ge(s.sw, i + 1)
                    reused(pe, s.relu, i, 1)
                    for k in range(G):
                        last = pe.matmul(tile(PS[2], k), tile(WC2[:, par], k), cols(AT, i, GW, k * T, T),
                                         start=True, stop=True)
                    last.then_inc(s.conv, 1)

                def back(i, par, half):
                    pe.wait_ge(s.relu, i + 1)
                    reused(pe, s.x1, i, 1)
                    transpose4(pe, PS[3], WD[:, par], s.back)

                def feat(i, par, half):
                    pe.wait_ge(s.xn2, i + 1)
                    reused(pe, s.f, i, 1)
                    transpose4(pe, PS[4], WE[:, par], s.f_ps)

                def logits(i, par, half):
                    pe.wait_ge(s.f, i + 1)
                    reused(pe, s.lg, i, 1)
                    for k in range(G):
                        last = pe.matmul(PS[5][:, k * E3:(k + 1) * E3], tile(WF[:, par], k), rw3[:], start=True, stop=True)
                    last.then_inc(s.lg_ps, 1)

                def hot(i, par, half):
                    pe.wait_ge(s.hot, i + 1)
                    reused(pe, s.hot_T, i, 1)
                    for k in range(G):
                        last = pe.transpose(PS[6][0:E3, k * T:(k + 1) * T], HOT[:, par, k, :], ident[:])
                    last.then_inc(s.hT_ps, 1)
                pe.wait_ge(s.w, 5 * 16)
                pe.wait_ge(s.dws, 1)
                pipelined(pe, NG, [(2, conv), (1, xT), (4, logits), (1, support), (2, back), (3, feat), (5, hot)])

            @block.scalar
            def _(act):
                def xT(i, par, half):
                    act.wait_ge(s.x_ps, i + 1)
                    reused(act, s.sw_ps, i, 2)
                    act.copy(WB[:, par], PS[0]).then_inc(s.xT, 1)

                def support(i, par, half):
                    act.wait_ge(s.sw_ps, i + 1)
                    reused(act, s.conv, i, 2)
                    act.copy(WC2[:, par], PS[1]).then_inc(s.sw, 1)

                def relu(i, par, half):
                    act.wait_ge(s.conv, i + 1)
                    reused(act, s.back, i, 2)
                    act.activation(WD[:, par], PS[2], ACT.Relu, bias=b3g[:]).then_inc(s.relu, 1)

                def feat(i, par, half):
                    act.wait_ge(s.f_ps, i + 1)
                    reused(act, s.keep, i, 2)
                    reused(act, s.lg_ps, i, 2)
                    act.copy(WF[:, par], PS[4]).then_inc(s.f, 1)

                def hot(i, par, half):
                    act.wait_ge(s.hT_ps, i + 1)
                    act.copy(cols(HOT_T, i), PS[6][0:E3, :]).then_inc(s.hot_T, 1)
                act.wait_ge(s.w, 5 * 16)
                pipelined(act, NG, [(2, relu), (1, xT), (1, support), (3, feat), (5, hot)])

            @block.vector
            def _(v):
                def stats(i, par, half):
                    statistics(v, i, par, STATS, MV, s.raw, s.mv)

                def norm(i, par, half):
                    v.wait_ge(s.rstd, i + 1)
                    reused(v, s.x_ps, i, 2)
                    normalise(v, i, par, WA, MV, RS, 1, s.xn)

                def add(i, par, half):
                    v.wait_ge(s.back, i + 1)
                    v.tensor_tensor(cols(X, i), cols(X, i), PS[3], ALU.add).then_inc(s.x1, 1)
                    wait_apart(v, s.x1, i + 1)
                    statistics(v, i, par, STATSB, MVB, s.raw2, s.mv2)

                def norm2(i, par, half):
                    v.wait_ge(s.rstd2, i + 1)
                    reused(v, s.f_ps, i, 2)
                    normalise(v, i, par, WE, MVB, RSB, 1, s.xn2)

                def top(i, par, half):
                    v.wait_ge(s.lg_ps, i + 1)
                    v.tensor_tensor(LG3[:, par], PS[5][:, 0:G * E3].rearrange("p (g e) -> p g e", g=G),
                                    rb3[:].unsqueeze(1).to_broadcast([P, G, E3]), ALU.add).then_inc(s.lg, 1)
                    wait_apart(v, s.lg, i + 1)
                    for k in range(G):
                        last = v.max(TOP3[:, par, k, :], LG3[:, par, k, :])
                    last.then_inc(s.top, 1)
                    wait_apart(v, s.top, i + 1)
                    for k in range(G):
                        last = v.max_index(IDX3[:, par, k, :], TOP3[:, par, k, :], LG3[:, par, k, :])
                    last.then_inc(s.idx, 1)
                    v.wait_ge(s.idx, i + 1)
                    v.tensor_copy(IDXG3[:, par], IDX3[:, par]).then_inc(s.idf, 1)
                    v.wait_ge(s.idf, i + 1)
                    reused(v, s.hT_ps, i, 2)
                    for k in range(G):
                        last = v.tensor_scalar(HOT[:, par, k, :], iota32[:], IDXG3[:, par, k, 0:1], None, ALU.is_equal)
                    last.then_inc(s.hot, 1)
                v.wait_ge(s.w, 5 * 16)
                v.tensor_scalar(dw[:], w3[:], SPARSITY, None, ALU.is_gt).then_inc(s.pos, 1)
                v.tensor_scalar(dwn[:], w3[:], -SPARSITY, None, ALU.is_lt).then_inc(s.neg, 1)
                v.wait_ge(s.neg, 1)
                v.wait_ge(s.pos, 1)
                v.tensor_tensor(w3[:], dw[:], dwn[:], ALU.subtract).then_inc(s.dw, 1)
                v.wait_ge(s.dw, 1)
                v.tensor_scalar(dw[:], w3[:], SPARSITY, None, ALU.mult).then_inc(s.dws, 1)
                v.wait_ge(s.g1, 1)
                pipelined(v, NG, [(3, norm2), (1, norm), (0, stats), (2, add), (4, top)])

        s = sems("ex3", "w gb g1 g2 h_ps h hid y back x1")
        HID = E3 * F3
        W1_3 = EXP[:, 0:HID].rearrange("p (c n) -> p c n", c=C3)
        W2_3 = EXP[:, HID:2 * HID].rearrange("p (c d) -> p c d", c=C3)
        GATE = EXP[0:E3, 2 * HID:3 * HID]
        H3 = EXP[:, 3 * HID:3 * HID + 4 * GW].rearrange("p (a n) -> p a n", a=4)
        with nc.Block() as block:
            @block.sync
            def _(sp):
                sp.dma_start(W1_3.rearrange("p c (e f) -> p (c e) f", e=EC3), a["L3_ffn_W1"].rearrange("e d f -> d e f")
                             ).then_inc(s.w, 16)
                sp.dma_start(W2_3, a["L3_ffn_W2"].rearrange("(c e) f d -> (e f) c d", c=C3)).then_inc(s.w, 16)
                sp.dma_start(GATE, a["L3_ffn_b1"].rearrange("e f -> (e f)").partition_broadcast(E3)).then_inc(s.gb, 16)

            @block.gpsimd
            def _(pool):
                pool.wait_ge(s.gb, 16)
                pool.affine_select(out=GATE, in_=GATE, compare_op=ALU.is_ge, fill=NONE, base=0, pattern=[[1, HID]],
                                   channel_multiplier=-F3).then_inc(s.g1, 1)
                pool.wait_ge(s.g1, 1)
                pool.affine_select(out=GATE, in_=GATE, compare_op=ALU.is_ge, fill=NONE, base=F3 - 1, pattern=[[-1, HID]],
                                   channel_multiplier=F3).then_inc(s.g2, 1)

            @block.tensor
            def _(pe):
                def up(i, c):
                    u = i * C3 + c
                    reused(pe, s.h, u, 4) if isinstance(i, int) else pe.wait_ge(s.h, u - 3)
                    bank = PS[c % 4]
                    pe.matmul(bank, W1_3[:, c, :], cols(FEAT, i), start=True, stop=False)
                    pe.matmul(bank, GATE[:, c * P:(c + 1) * P], cols(HOT_T, i), start=False, stop=True).then_inc(s.h_ps, 1)

                def down(i, c, par):
                    pe.wait_ge(s.h, i * C3 + c + 1)
                    if c == 0:
                        reused(pe, s.y, i, 2)
                    last = pe.matmul(PS[4 + par], W2_3[:, c, :], H3[:, c % 4, :], start=(c == 0), stop=False)
                    if c == C3 - 1:
                        last = pe.matmul(PS[4 + par], b2_3[:], cols(HOT_T, i), start=False, stop=True)
                    last.then_inc(s.hid, 1)

                def group(i, par, half):
                    for c in range(C3):
                        up(i, c)
                        if c >= 2:
                            down(i, c - 2, par)
                        elif not (isinstance(i, int) and i == 0):
                            down(i - 1, C3 - 2 + c, 1 - par)

                def back(i, par, half):
                    if isinstance(i, int) and i == NG - 1:
                        for c in (C3 - 2, C3 - 1):
                            down(i, c, par)
                    pe.wait_ge(s.y, i + 1)
                    reused(pe, s.x1, i, 1)
                    transpose4(pe, PS[6], WD[:, par], s.back)
                pe.wait_ge(s.w, 32)
                pe.wait_ge(s.g2, 1)
                pipelined(pe, NG, [(0, group), (1, back)])

            @block.scalar
            def _(act):
                def hidden(i, c):
                    u = i * C3 + c
                    act.wait_ge(s.h_ps, u + 1)
                    reused(act, s.hid, u, 4) if isinstance(i, int) else act.wait_ge(s.hid, u - 3)
                    act.activation(H3[:, c % 4, :], PS[c % 4], ACT.Relu).then_inc(s.h, 1)

                def group(i, par, half):
                    for c in range(C3):
                        hidden(i, c)
                        if c == 2 and not (isinstance(i, int) and i == 0):
                            result(i - 1, 1 - par)

                def result(i, par):
                    act.wait_ge(s.hid, (i + 1) * C3)
                    reused(act, s.back, i, 2)
                    act.activation(WD[:, par], PS[4 + par], ACT.Relu).then_inc(s.y, 1)
                act.wait_ge(s.w, 32)
                pipelined(act, NG, [(0, group)])
                result(NG - 1, (NG - 1) % 2)

            @block.vector
            def _(v):
                def add(i, par, half):
                    v.wait_ge(s.back, i + 1)
                    v.tensor_tensor(cols(X, i), cols(X, i), PS[6], ALU.add).then_inc(s.x1, 1)
                pipelined(v, NG, [(0, add)])

        s = sems("out", "stored")
        out_v = out.rearrange("(g b) t h -> g t b h", b=G)
        with nc.Block() as block:
            @block.sync
            def _(sp):
                for g in range(0, NG, 4):
                    sp.dma_start(out.rearrange("b t h -> t b h")[:, G * g:G * (g + 4), :],
                                 X[:, g * GW:(g + 4) * GW].rearrange("p (b h) -> p b h", h=H)).then_inc(s.stored, 16)
                sp.wait_ge(s.stored, 16 * (NG // 4))
        release()
        layer()


def kernel(**inputs):
    import numpy as np
    import concourse.bacc as bacc
    from concourse.bass_utils import run_bass_kernel_spmd

    nc = bacc.Bacc("TRN2", target_bir_lowering=False, num_devices=1)
    arrays, aps = {}, {}
    for name, value in inputs.items():
        v = np.ascontiguousarray(value)
        arrays["in_" + name] = v
        aps[name] = nc.dram_tensor("in_" + name, v.shape, mybir.dt.from_np(v.dtype), kind="ExternalInput").ap()
    b1 = np.ascontiguousarray(np.asarray(inputs["L1_ffn_b1"]).reshape(E1 * C1, P).T)
    arrays["in_L1_ffn_b1_T"] = b1
    aps["L1_ffn_b1_T"] = nc.dram_tensor("in_L1_ffn_b1_T", b1.shape, FP32, kind="ExternalInput").ap()
    for name in ("Wq", "Wk", "Wv", "Wo"):
        wt = np.ascontiguousarray(np.asarray(inputs["L2_gnn_" + name]).T)
        arrays[f"in_L2_gnn_{name}_T"] = wt
        aps[f"L2_gnn_{name}_T"] = nc.dram_tensor(f"in_L2_gnn_{name}_T", wt.shape, FP32, kind="ExternalInput").ap()
    for name, shape in (("L2_ffn_b1p", (E2 * C2, P)), ("L2_ffn_b1s", (C2, P)), ("L3_ffn_router_w", (E3, H))):
        wt = np.ascontiguousarray(np.asarray(inputs[name]).reshape(shape).T)
        arrays[f"in_{name}_T"] = wt
        aps[f"{name}_T"] = nc.dram_tensor(f"in_{name}_T", wt.shape, FP32, kind="ExternalInput").ap()
    out = nc.dram_tensor("out_x", (B, T, H), FP32, kind="ExternalOutput").ap()
    program(nc, aps, out)
    return run_bass_kernel_spmd(nc, [arrays], core_ids=[0]).results[0]["out_x"]
```
